# Optimizing a Trainium2 kernel written in Bass

```python
import numpy as np
import jax
import jax.numpy as jnp

def _softmax(x, axis=-1):
    return jax.nn.softmax(x, axis=axis)

def _gelu(x):
    return jax.nn.gelu(x, approximate=True)

def _silu(x):
    return jax.nn.silu(x)

def _sigmoid(x):
    return jax.nn.sigmoid(x)

def _layernorm(x, axis=-1, eps=1e-05):
    m = jnp.mean(x, axis=axis, keepdims=True)
    v = jnp.var(x, axis=axis, keepdims=True)
    return (x - m) / jnp.sqrt(v + eps)

def _scatter_add(tgt, idx, src, axis=0):
    return tgt.at[idx].add(src)

def _segment_sum(src, seg, n):
    return jax.ops.segment_sum(src, seg, n)
kernel_name = 'mk_cond_seq_d2_seqx_r4_04b5e0'

def setup_inputs(seed: int=0):
    np.random.seed(seed)
    _w = jnp.asarray

    def _rec_inputs():
        import jax
        import jax.numpy as jnp
        _rk = jax.random.key(seed)
        x = 7.22e-05 + 1 * jax.random.normal(jax.random.fold_in(_rk, 1), (2, 1024, 256), jnp.float32)
        _lenS = 1024 - jax.random.randint(jax.random.fold_in(_rk, 7), (2,), 0, max(1, 1024 // 4) + 1, jnp.int32)
        _lenS2 = 1024 - jax.random.randint(jax.random.fold_in(_rk, 8), (2,), 0, max(1, 1024 // 4) + 1, jnp.int32)
        cond_1024 = 0.00782532 + 1.00527 * jax.random.normal(jax.random.fold_in(_rk, 11), (2, 256), jnp.float32)
        _validS = jnp.arange(1024)[None, :] < _lenS[:, None]
        _validS2 = jnp.arange(1024)[None, :] < _lenS2[:, None]
        _causal = jnp.tril(jnp.ones((1024, 1024), dtype=bool))
        mask_BxS_bk1 = jnp.broadcast_to(_validS[:, :], (2, 1024))
        return (x, cond_1024, mask_BxS_bk1)
    x, cond_1024, mask_BxS_bk1 = _rec_inputs()

    def _L0_cond_setup():
        import jax, jax.numpy as jnp
        import numpy as np
        B, N, C = (8, 256, 256)
        H = 16
        HD = C // H
        MLP = 4 * C
        EPS = 1e-06

        def _layernorm(x):
            mu = jnp.mean(x, axis=-1, keepdims=True)
            var = jnp.mean((x - mu) ** 2, axis=-1, keepdims=True)
            return (x - mu) * jax.lax.rsqrt(var + EPS)

        def _modulate(x, shift, scale):
            return x * (1.0 + scale[:, None, :]) + shift[:, None, :]

        def _attention(x, padding_mask, qkv_w, qkv_b, proj_w, proj_b):
            b, n, cdim = x.shape
            qkv = x @ qkv_w.T + qkv_b
            qkv = qkv.reshape(b, n, 3, H, HD).transpose(2, 0, 3, 1, 4)
            q, k, v = (qkv[0], qkv[1], qkv[2])
            scale = HD ** (-0.5)
            attn = jnp.einsum('bhnd,bhmd->bhnm', q, k) * scale
            mask = padding_mask[:, None, :] & padding_mask[:, :, None]
            attn = jnp.where(mask[:, None, :, :], attn, -1000000000.0)
            attn = jax.nn.softmax(attn, axis=-1)
            out = jnp.einsum('bhnm,bhmd->bhnd', attn, v)
            out = out.transpose(0, 2, 1, 3).reshape(b, n, cdim)
            return out @ proj_w.T + proj_b
        key = jax.random.key(seed)
        ks = jax.random.split(key, 12)
        x = jax.random.normal(ks[0], (B, N, C), dtype=jnp.float32)
        c = jax.random.normal(ks[1], (B, C), dtype=jnp.float32)
        lengths = jax.random.randint(ks[2], (B,), N // 2, N + 1)
        padding_mask = jnp.arange(N)[None, :] < lengths[:, None]
        s = 0.02
        qkv_w = jax.random.normal(ks[3], (3 * C, C), dtype=jnp.float32) * s
        qkv_b = jnp.zeros((3 * C,), dtype=jnp.float32)
        proj_w = jax.random.normal(ks[4], (C, C), dtype=jnp.float32) * s
        proj_b = jnp.zeros((C,), dtype=jnp.float32)
        fc1_w = jax.random.normal(ks[5], (MLP, C), dtype=jnp.float32) * s
        fc1_b = jnp.zeros((MLP,), dtype=jnp.float32)
        fc2_w = jax.random.normal(ks[6], (C, MLP), dtype=jnp.float32) * s
        fc2_b = jnp.zeros((C,), dtype=jnp.float32)
        ada_w = jax.random.normal(ks[7], (6 * C, C), dtype=jnp.float32) * s
        ada_b = jnp.zeros((6 * C,), dtype=jnp.float32)
        return {'x': x, 'c': c, 'padding_mask': padding_mask, 'qkv_w': qkv_w, 'qkv_b': qkv_b, 'proj_w': proj_w, 'proj_b': proj_b, 'fc1_w': fc1_w, 'fc1_b': fc1_b, 'fc2_w': fc2_w, 'fc2_b': fc2_b, 'ada_w': ada_w, 'ada_b': ada_b}
    _L0_cond_all = _L0_cond_setup()
    _L0_cond_in = {k: v for k, v in _L0_cond_all.items() if k in ('qkv_w', 'qkv_b', 'proj_w', 'proj_b', 'fc1_w', 'fc1_b', 'fc2_w', 'fc2_b', 'ada_w', 'ada_b')}
    del _L0_cond_all

    def _L1_cond_setup():
        import jax, jax.numpy as jnp
        import numpy as np
        EPS = 1e-05

        def _sln(h, w, ln_g, ln_b, Wg, bg, Wb, bb):
            mu = jnp.mean(h, axis=-1, keepdims=True)
            var = jnp.mean((h - mu) ** 2, axis=-1, keepdims=True)
            ln = (h - mu) / jnp.sqrt(var + EPS) * ln_g + ln_b
            gamma = (w @ Wg.T + bg)[:, None, :]
            beta = (w @ Wb.T + bb)[:, None, :]
            return gamma * ln + beta
        key = jax.random.key(seed)
        ks = jax.random.split(key, 20)
        B, N, D = (4, 256, 256)
        F = 4 * D
        s = lambda fan: 1.0 / np.sqrt(fan)
        inp = {'hidden': jax.random.normal(ks[0], (B, N, D), jnp.float32), 'w': jax.random.normal(ks[1], (B, D), jnp.float32), 'ln_g': jnp.ones((D,), jnp.float32), 'ln_b': jnp.zeros((D,), jnp.float32), 'Wg': jax.random.normal(ks[2], (D, D), jnp.float32) * s(D), 'bg': jnp.zeros((D,), jnp.float32), 'Wb': jax.random.normal(ks[3], (D, D), jnp.float32) * s(D), 'bb': jnp.zeros((D,), jnp.float32), 'Wqkv': jax.random.normal(ks[4], (3 * D, D), jnp.float32) * s(D), 'bqkv': jnp.zeros((3 * D,), jnp.float32), 'Wp': jax.random.normal(ks[5], (D, D), jnp.float32) * s(D), 'bp': jnp.zeros((D,), jnp.float32), 'W1': jax.random.normal(ks[6], (F, D), jnp.float32) * s(D), 'b1': jnp.zeros((F,), jnp.float32), 'W2': jax.random.normal(ks[7], (D, F), jnp.float32) * s(F), 'b2': jnp.zeros((D,), jnp.float32), 'num_heads': 16}
        return inp
    _L1_cond_all = _L1_cond_setup()
    _L1_cond_in = {k: v for k, v in _L1_cond_all.items() if k in ('ln_g', 'ln_b', 'Wg', 'bg', 'Wb', 'bb', 'Wqkv', 'bqkv', 'Wp', 'bp', 'W1', 'b1', 'W2', 'b2')}
    del _L1_cond_all
    return {'x': x, 'cond_1024': cond_1024, 'mask_BxS_bk1': mask_BxS_bk1, 'L0_cond_qkv_w': _L0_cond_in['qkv_w'], 'L0_cond_qkv_b': _L0_cond_in['qkv_b'], 'L0_cond_proj_w': _L0_cond_in['proj_w'], 'L0_cond_proj_b': _L0_cond_in['proj_b'], 'L0_cond_fc1_w': _L0_cond_in['fc1_w'], 'L0_cond_fc1_b': _L0_cond_in['fc1_b'], 'L0_cond_fc2_w': _L0_cond_in['fc2_w'], 'L0_cond_fc2_b': _L0_cond_in['fc2_b'], 'L0_cond_ada_w': _L0_cond_in['ada_w'], 'L0_cond_ada_b': _L0_cond_in['ada_b'], 'L1_cond_ln_g': _L1_cond_in['ln_g'], 'L1_cond_ln_b': _L1_cond_in['ln_b'], 'L1_cond_Wg': _L1_cond_in['Wg'], 'L1_cond_bg': _L1_cond_in['bg'], 'L1_cond_Wb': _L1_cond_in['Wb'], 'L1_cond_bb': _L1_cond_in['bb'], 'L1_cond_Wqkv': _L1_cond_in['Wqkv'], 'L1_cond_bqkv': _L1_cond_in['bqkv'], 'L1_cond_Wp': _L1_cond_in['Wp'], 'L1_cond_bp': _L1_cond_in['bp'], 'L1_cond_W1': _L1_cond_in['W1'], 'L1_cond_b1': _L1_cond_in['b1'], 'L1_cond_W2': _L1_cond_in['W2'], 'L1_cond_b2': _L1_cond_in['b2']}

def reference(x, cond_1024, mask_BxS_bk1, L0_cond_qkv_w, L0_cond_qkv_b, L0_cond_proj_w, L0_cond_proj_b, L0_cond_fc1_w, L0_cond_fc1_b, L0_cond_fc2_w, L0_cond_fc2_b, L0_cond_ada_w, L0_cond_ada_b, L1_cond_ln_g, L1_cond_ln_b, L1_cond_Wg, L1_cond_bg, L1_cond_Wb, L1_cond_bb, L1_cond_Wqkv, L1_cond_bqkv, L1_cond_Wp, L1_cond_bp, L1_cond_W1, L1_cond_b1, L1_cond_W2, L1_cond_b2):
    import jax
    import jax.numpy as jnp

    def _L0_cond_ref(x, c, padding_mask, qkv_w, qkv_b, proj_w, proj_b, fc1_w, fc1_b, fc2_w, fc2_b, ada_w, ada_b):
        import jax, jax.numpy as jnp
        import numpy as np
        B, N, C = (8, 256, 256)
        H = 16
        HD = C // H
        MLP = 4 * C
        EPS = 1e-06

        def _layernorm(x):
            mu = jnp.mean(x, axis=-1, keepdims=True)
            var = jnp.mean((x - mu) ** 2, axis=-1, keepdims=True)
            return (x - mu) * jax.lax.rsqrt(var + EPS)

        def _modulate(x, shift, scale):
            return x * (1.0 + scale[:, None, :]) + shift[:, None, :]

        def _attention(x, padding_mask, qkv_w, qkv_b, proj_w, proj_b):
            b, n, cdim = x.shape
            qkv = x @ qkv_w.T + qkv_b
            qkv = qkv.reshape(b, n, 3, H, HD).transpose(2, 0, 3, 1, 4)
            q, k, v = (qkv[0], qkv[1], qkv[2])
            scale = HD ** (-0.5)
            attn = jnp.einsum('bhnd,bhmd->bhnm', q, k) * scale
            mask = padding_mask[:, None, :] & padding_mask[:, :, None]
            attn = jnp.where(mask[:, None, :, :], attn, -1000000000.0)
            attn = jax.nn.softmax(attn, axis=-1)
            out = jnp.einsum('bhnm,bhmd->bhnd', attn, v)
            out = out.transpose(0, 2, 1, 3).reshape(b, n, cdim)
            return out @ proj_w.T + proj_b
        mod = jax.nn.silu(c) @ ada_w.T + ada_b
        shift_msa, scale_msa, gate_msa, shift_mlp, scale_mlp, gate_mlp = jnp.split(mod, 6, axis=1)
        h = _modulate(_layernorm(x), shift_msa, scale_msa)
        x = x + gate_msa[:, None, :] * _attention(h, padding_mask, qkv_w, qkv_b, proj_w, proj_b)
        h = _modulate(_layernorm(x), shift_mlp, scale_mlp)
        h = jax.nn.gelu(h @ fc1_w.T + fc1_b, approximate=True) @ fc2_w.T + fc2_b
        x = x + gate_mlp[:, None, :] * h
        return x

    def _L1_cond_ref(hidden, w, ln_g, ln_b, Wg, bg, Wb, bb, Wqkv, bqkv, Wp, bp, W1, b1, W2, b2, num_heads):
        import jax, jax.numpy as jnp
        import numpy as np
        EPS = 1e-05

        def _sln(h, w, ln_g, ln_b, Wg, bg, Wb, bb):
            mu = jnp.mean(h, axis=-1, keepdims=True)
            var = jnp.mean((h - mu) ** 2, axis=-1, keepdims=True)
            ln = (h - mu) / jnp.sqrt(var + EPS) * ln_g + ln_b
            gamma = (w @ Wg.T + bg)[:, None, :]
            beta = (w @ Wb.T + bb)[:, None, :]
            return gamma * ln + beta
        B, N, D = hidden.shape
        hd = D // num_heads
        h = _sln(hidden, w, ln_g, ln_b, Wg, bg, Wb, bb)
        qkv = (h @ Wqkv.T + bqkv).reshape(B, N, num_heads, hd, 3)
        q = jnp.moveaxis(qkv[..., 0], 2, 1)
        k = jnp.moveaxis(qkv[..., 1], 2, 1)
        v = jnp.moveaxis(qkv[..., 2], 2, 1)
        energy = jnp.einsum('bhqd,bhkd->bhqk', q, k)
        att = jax.nn.softmax(energy, axis=-1) / D ** 0.5
        out = jnp.einsum('bhqk,bhkd->bhqd', att, v)
        out = jnp.moveaxis(out, 1, 2).reshape(B, N, D)
        out = out @ Wp.T + bp
        h1 = out + hidden
        h2 = _sln(h1, w, ln_g, ln_b, Wg, bg, Wb, bb)
        return h2 + h1
    x = _L0_cond_ref(x, cond_1024, mask_BxS_bk1, L0_cond_qkv_w, L0_cond_qkv_b, L0_cond_proj_w, L0_cond_proj_b, L0_cond_fc1_w, L0_cond_fc1_b, L0_cond_fc2_w, L0_cond_fc2_b, L0_cond_ada_w, L0_cond_ada_b)
    x = _L1_cond_ref(x, cond_1024, L1_cond_ln_g, L1_cond_ln_b, L1_cond_Wg, L1_cond_bg, L1_cond_Wb, L1_cond_bb, L1_cond_Wqkv, L1_cond_bqkv, L1_cond_Wp, L1_cond_bp, L1_cond_W1, L1_cond_b1, L1_cond_W2, L1_cond_b2, 16)
    return x

_drawn_inputs = setup_inputs


def setup_inputs(seed=0):
    import zlib

    import numpy as np

    out = dict(_drawn_inputs(seed))
    spreads = {'L0_cond_qkv_b': (0.0, 0.8),
     'L0_cond_proj_b': (0.0, 0.368),
     'L0_cond_fc1_b': (0.0, 0.8),
     'L0_cond_fc2_b': (0.0, 0.493),
     'L0_cond_ada_b': (0.0, 0.518),
     'L1_cond_ln_g': (1.0, 0.2),
     'L1_cond_ln_b': (0.0, 0.338),
     'L1_cond_bg': (0.0, 0.351),
     'L1_cond_bb': (0.0, 0.352),
     'L1_cond_bqkv': (0.0, 2.0),
     'L1_cond_bp': (0.0, 0.377),
     'L1_cond_b1': (0.0, 0.1),
     'L1_cond_b2': (0.0, 0.1)}
    factors = {'L0_cond_qkv_w': 8.0, 'L0_cond_proj_w': 8.0, 'L0_cond_fc1_w': 2.688, 'L1_cond_Wqkv': 2.963}
    for name, (base, spread) in spreads.items():
        noise = np.random.default_rng([zlib.crc32(name.encode()), seed]).standard_normal(out[name].shape)
        drawn = base * np.exp(spread * noise) if base else spread * noise
        out[name] = jnp.asarray(drawn.astype(out[name].dtype))
    for name, factor in factors.items():
        out[name] = (out[name] * factor).astype(out[name].dtype)
    return out
```

```python
from contextlib import ExitStack

import concourse.bass as bass
from concourse import mybir

ALU = mybir.AluOpType
ACT = mybir.ActivationFunctionType
AX = mybir.AxisListType
F32 = mybir.dt.float32
BF16 = mybir.dt.bfloat16
U8 = mybir.dt.uint8

P = 128
B, N, C = 2, 1024, 256
H, HD = 16, 16
MLP = 4 * C
TT = N // P
CC = C // P
HG = 4
GROUPS = H // HG
QW = 512
QH = N // QW
TQ = QW // P
KT = N // P
ITEMS = GROUPS * QH
FC = MLP // P
TB = 4
BW = N // TB
LAYERS = 2
UNITS = LAYERS * B
EPS = (1e-6, 1e-5)
MASKED = -float(2 ** 30)
PARTS_Q = (0, 0, 0, 1, 1, 2)
PARTS_K = (0, 1, 2, 0, 1, 0)
ROW_MASK = len(PARTS_Q) * HD
ROW_MAX = ROW_MASK + 1
ROWS = ROW_MAX + 3
VW = HD + 1
CW = 32
SLOTS = 3

COLS = dict(qk0=0, qk1=4, fc1=8, mod=16, lng=28, lnb=30)
NCOLS = 32
ROWV = ("v0", "v1", "proj0", "proj1", "fc2", "gate_msa", "gate_mlp", "gamma", "beta", "ln_g", "ln_b")


def schedule():
    plan = [("mod",)] + [("rows", b, k) for b in range(B) for k in range(4)]

    def norm(u, k):
        plan.append(("stats", u, k))
        for th in range(2):
            plan.append(("xn", u, k, th))
            plan.extend(("lnT", u, k, th, cc) for cc in range(CC))

    def scores_max(u, i, s):
        plan.extend(("smax", u, i, 4 * s + k) for k in range(4))
        if s == 7:
            plan.append(("neg", u, i))
            plan.append(("mrow", u, i))

    for u in range(UNITS):
        layer = u // B
        norm(u, 0)
        plan.extend(("qk", u, j) for j in (0, 1, 4, 5, 2, 3, 6, 7))
        plan.append(("bias_in", u, 0))
        plan.extend(("v", u, t) for t in range(TT))
        for i in range(2):
            for s in range(8):
                scores_max(u, i, s)
        for i in range(ITEMS):
            for s in range(8):
                plan.append(("st", u, i, s, 0))
                plan.append(("st", u, i, s, 1))
                if i + 2 < ITEMS:
                    plan.append(("smax", u, i + 2, 4 * s))
                plan.append(("st", u, i, s, 2))
                plan.append(("st", u, i, s, 3))
                if i + 2 < ITEMS:
                    plan.append(("smax", u, i + 2, 4 * s + 1))
                if s > 0:
                    plan.append(("pv", u, i, s - 1))
                elif i > 0:
                    plan.append(("pv", u, i - 1, 7))
                    plan.append(("evac", u, i - 1))
                if i + 2 < ITEMS:
                    plan.append(("smax", u, i + 2, 4 * s + 2))
                    plan.append(("smax", u, i + 2, 4 * s + 3))
                if s == 1 and i > 0:
                    plan.append(("oT", u, i - 1))
                if s == 7 and i + 2 < ITEMS:
                    plan.append(("neg", u, i + 2))
                if s == 2 and 0 < i and i + 1 < ITEMS:
                    plan.append(("mrow", u, i + 1))
        plan.append(("pv", u, ITEMS - 1, 7))
        plan.append(("evac", u, ITEMS - 1))
        plan.append(("oT", u, ITEMS - 1))
        plan.extend(("opT", u, th, cc) for th in range(2) for cc in range(CC))
        plan.extend(("proj", u, t) for t in range(TT))
        if layer == 0:
            norm(u, 1)
            plan.append(("bias_in", u, 1))
            for tb in range(TB):
                plan.extend(("fc1", u, tb, f) for f in range(FC // 2))
                plan.extend(("fc2", u, tb, t) for t in range(2))
        else:
            plan.append(("stats", u, 1))
            plan.extend(("fin", u, t) for t in range(TT))
    fixed = []
    for e in plan:
        fixed.append(e)
    return fixed


def taker(e):
    kind = e[0]
    if kind in ("mod", "rows", "v", "oT", "proj", "fc2"):
        return "dve"
    if kind == "qk":
        return "dve" if e[1] // B == 0 and e[2] < 4 else "act"
    if kind in ("lnT", "mrow", "opT", "fc1"):
        return "act"
    return None


def build(nc, x, cT, mask, adaT, WgT, WbT, qkvT0, qkvT1, projT0, projT1, fc1T, fc2T, cols, rows, out):
    plan = schedule()
    jobs, taken = {}, {"dve": 0, "act": 0}
    order = []
    for e in plan:
        if (w := taker(e)) is not None:
            taken[w] += 1
            jobs[e] = (len(order), w, taken[w])
            order.append(e)

    def count(kind, *before):
        n = 0
        for e in plan:
            if e[0] == kind:
                n += 1
                if e == (kind, *before):
                    return n
        raise ValueError((kind, before))

    counts = {}
    seen = {}
    for e in plan:
        seen[e[0]] = seen.get(e[0], 0) + 1
        counts[e] = seen[e[0]]

    scratch = nc.dram_tensor("qk_parts", (2, 2, 3, C, N), BF16, kind="Internal").ap()

    mask_rows = nc.dram_tensor("mask_rows", (3, 2, N), BF16, kind="Internal").ap()

    with ExitStack() as ctx:
        def sb(name, shape, dt=F32):
            return ctx.enter_context(nc.sbuf_tensor(name, shape, dt))

        def bank(name):
            return ctx.enter_context(nc.psum_tensor(name, [P, 512], F32))

        def sem(name):
            return ctx.enter_context(nc.semaphore(name))

        xs = sb("xs", [P, B * TT, C])
        xn = sb("xn", [P, 4, C])
        stat = sb("stat", [P, TT, 6])
        mv = sb("mv", [P, TT, 2])
        rstd = sb("rstd", [P, 2, TT])
        power = sb("power", [P, TT])
        hT = sb("hT", [P, CC, N])
        qf = sb("qf", [P, 2, 512])
        parts = sb("parts", [P, 2, 3, 512], BF16)
        qs = [sb(f"qs{i}", [P, HG, N], BF16) for i in range(SLOTS)]
        ks = [sb(f"ks{i}", [P, HG, N], BF16) for i in range(SLOTS)]
        va = sb("va", [P, KT, H, VW])
        prob = sb("prob", [P, 2, HG, QW])
        mx = sb("mx", [P, 2, HG * TQ, 2])
        negm = sb("negm", [P, 2, HG * TQ])
        mpart = sb("mpart", [P, 2, 3, HG * TQ], BF16)
        mrow = sb("mrow", [3 * HG, 2, QW], BF16)
        oraw = sb("oraw", [P, 2, QW])
        rec = sb("rec", [P, 2, TQ, HG])
        otok = sb("otok", [P, TT, C])
        oT = sb("oT", [P, CC, N])
        tmp = sb("tmp", [P, 2, C])
        ge = sb("ge", [P, FC, BW])
        wqkv = [sb(f"wqkv{i}", [P, CC, 3 * C]) for i in range(LAYERS)]
        wproj = [sb(f"wproj{i}", [P, CC, C]) for i in range(LAYERS)]
        wfc1 = sb("wfc1", [P, CC, MLP])
        wfc2 = sb("wfc2", [P, FC, C])
        col = sb("col", [P, NCOLS])
        row = sb("row", [P, len(ROWV), C])
        gate = sb("gate", [P, B, 4, C])
        gbias = sb("gbias", [P, B, 2, C])
        modc = sb("modc", [P, 12, B])
        l1c = sb("l1c", [P, 4, B])
        cs = sb("cs", [P, CC, B])
        sig = sb("sig", [P, 2, CC, B])
        sc = sb("sc", [P, CC, B])
        vq = sb("vq", [P, B, N], BF16)
        idf = sb("idf", [P, P])
        idb = sb("idb", [P, P], BF16)
        wada = prob[:, :, :, :].rearrange("p a h q -> p (a h q)")[:, 0:CC * 6 * C].rearrange("p (k n) -> p k n", k=CC)
        gef = ge[:, :, :].rearrange("p f t -> p (f t)")
        wg = gef[:, 0:512].rearrange("p (k n) -> p k n", k=CC)
        wb = gef[:, 512:1024].rearrange("p (k n) -> p k n", k=CC)
        scB = gef[:, 1024:1536].rearrange("p (k b n) -> p k b n", k=CC, b=B)
        cB = gef[:, 1536:2048].rearrange("p (k b n) -> p k b n", k=CC, b=B)

        m8 = xn[:, :, :].rearrange("p t c -> p (t c)").bitcast(U8)[:, 0:B * N].rearrange("p (b n) -> p b n", b=B)
        mk8 = xn[:, :, :].rearrange("p t c -> p (t c)").bitcast(U8)[0:B, B * N:(B + 1) * N]
        mk = otok[:, :, :].rearrange("p t c -> p (t c)").bitcast(BF16)[0:3, 0:2 * N].rearrange("p (s n) -> p s n", s=2)

        A = [bank(f"A{i}") for i in range(3)]
        acc = bank("acc")
        M = [bank(f"M{i}") for i in range(2)]
        J = [bank(f"J{i}") for i in range(2)]

        s_x = [sem(f"s_x{b}") for b in range(B)]
        s_small = sem("s_small")
        s_ada = sem("s_ada")
        s_w = {n: sem(f"s_w_{n}") for n in ("qkv0", "qkv1", "proj0", "proj1", "fc1", "fc2")}
        s_id = sem("s_id")
        s_const = sem("s_const")
        s_ones = sem("s_ones")
        s_act0 = sem("s_act0")
        s_dve0 = sem("s_dve0")
        s_mask = sem("s_mask")
        s_acc = sem("s_acc")
        s_mrows = sem("s_mrows")
        s_modc = sem("s_modc")
        s_rows = sem("s_rows")
        job_full = sem("job_full")
        job_act = sem("job_act")
        job_dve = sem("job_dve")
        job_out = {"act": job_act, "dve": job_dve}
        dve_self = sem("dve_self")
        pool_self = sem("pool_self")
        stats_done = sem("stats_done")
        rstd_done = sem("rstd_done")
        xn_done = sem("xn_done")
        biased = sem("biased")
        parts_done = sem("parts_done")
        stored = [sem(f"stored{i}") for i in range(2)]
        loaded = [sem(f"loaded{i}") for i in range(SLOTS)]
        st_full = sem("st_full")
        exp_done = sem("exp_done")
        pv_done = sem("pv_done")
        acc_out = sem("acc_out")
        mx_full = sem("mx_full")
        mx_out = sem("mx_out")
        neg_done = sem("neg_done")
        mpart_done = sem("mpart_done")
        mrow_in = [sem(f"mrow_in{i}") for i in range(2)]
        fin_x = sem("fin_x")
        fin_out = sem("fin_out")
        s_out = [sem(f"s_out{k}") for k in range(4)]

        block = ctx.enter_context(nc.Block())

        def slot(u, g):
            return (u * GROUPS + g) % SLOTS

        def loads(u, g):
            return (u * GROUPS + g) // SLOTS + 1

        def item(u, i):
            return u * ITEMS + i

        def wait_bank(eng, e):
            n = jobs[e][0]
            if n >= 2:
                _, w, c = jobs[order[n - 2]]
                eng.wait_ge(job_out[w], c)
            return J[n % 2]

        def job_ready(eng, e):
            eng.wait_ge(job_full, jobs[e][0] + 1)
            return J[jobs[e][0] % 2]

        def job_taken(eng, e):
            _, w, c = jobs[e]
            eng.wait_ge(job_out[w], c)

        LOADS = 2 * len(PARTS_Q) + 2

        @block.sync
        def _(sp):
            for b in range(B):
                if b == 1:
                    sp.dma_start(wada, adaT.rearrange("(k p) n -> p k n", p=P)).then_inc(s_ada, 16)
                    sp.dma_start(wg, WgT.rearrange("(k p) n -> p k n", p=P)).then_inc(s_ada, 16)
                    sp.dma_start(wb, WbT.rearrange("(k p) n -> p k n", p=P)).then_inc(s_ada, 16)
                sp.dma_start(xs[:, b * TT:(b + 1) * TT, :], x[b].rearrange("(t p) c -> p t c", p=P)).then_inc(s_x[b], 16)
            for name, dst, src, k in (("qkv0", wqkv[0], qkvT0, CC), ("proj0", wproj[0], projT0, CC), ("fc1", wfc1, fc1T, CC),
                                      ("fc2", wfc2, fc2T, FC), ("qkv1", wqkv[1], qkvT1, CC), ("proj1", wproj[1], projT1, CC)):
                sp.dma_start(dst[:, :, :], src.rearrange("(k p) n -> p k n", p=P)).then_inc(s_w[name], 16)

            def store_parts(u, j):
                n = counts[("qk", u, j)]
                sp.wait_ge(parts_done, n)
                if u >= 2 and j == 0:
                    for g in range(GROUPS):
                        sp.wait_ge(loaded[slot(u - 2, g)], 16 * LOADS * loads(u - 2, g))
                side, cc, th = j // 4, j // 2 % 2, j % 2
                dst = scratch[u % 2, side, :, cc * P:(cc + 1) * P, th * 512:(th + 1) * 512]
                sp.dma_start(dst.rearrange("r c n -> c r n"), parts[:, (n - 1) % 2, :, :]).then_inc(stored[(n - 1) % 2], 16)

            def load_group(u, g):
                s = slot(u, g)
                jn = counts[("qk", u, 5 if g < 2 else 7)]
                for k in range(2):
                    sp.wait_ge(stored[k], 16 * (jn // 2))
                n = u * GROUPS + g
                if n >= SLOTS:
                    pu, pg = divmod(n - SLOTS, GROUPS)
                    sp.wait_ge(st_full, counts[("st", pu, 2 * pg + 1, 7, 3)])
                    sp.wait_ge(mx_full, counts[("smax", pu, 2 * pg + 1, 31)])
                rows_h = slice(g * HG * HD, (g + 1) * HG * HD)
                for dst, side, which in ((qs[s], 0, PARTS_Q), (ks[s], 1, PARTS_K)):
                    for r, part in enumerate(which):
                        sp.dma_start(dst[r * HD:(r + 1) * HD, :, :],
                                     scratch[u % 2, side, part, rows_h, :].rearrange("(h d) n -> d h n", d=HD)).then_inc(loaded[s], 16)
                kind = u if u < B else 2
                for side, dst in enumerate((qs[s], ks[s])):
                    sp.dma_start(dst[ROW_MASK:ROW_MASK + 1, :, :],
                                 mask_rows[kind:kind + 1, side:side + 1, :].to_broadcast([1, HG, N])).then_inc(loaded[s], 16)

            def put_max(u, i):
                e = ("mrow", u, i)
                job_taken(sp, e)
                s, qh = slot(u, i // 2), i % 2
                k = item(u, i) % 2
                for part in range(3):
                    sp.dma_start(qs[s][ROW_MAX + part:ROW_MAX + part + 1, :, qh * QW:(qh + 1) * QW],
                                 mrow[part * HG:(part + 1) * HG, k, :]).then_inc(mrow_in[k], 16)

            sp.wait_ge(s_mask, 1)
            sp.dma_start(mask_rows, mk).then_inc(s_mrows, 16)
            sp.wait_ge(s_mrows, 16)
            sp.wait_ge(s_ones, SLOTS)
            for e in plan:
                if e[0] == "qk":
                    store_parts(e[1], e[2])
                    if e[2] == 5:
                        load_group(e[1], 0)
                        load_group(e[1], 1)
                    if e[2] == 7:
                        load_group(e[1], 2)
                elif e[0] == "mrow":
                    put_max(e[1], e[2])
                elif e[0] == "fin":
                    _, u, t = e
                    sp.wait_ge(fin_x, counts[e])
                    sp.dma_start(out[u % B, t * P:(t + 1) * P, :], xn[:, t % 4, :]).then_inc(s_out[t % 4], 16)
                elif e[0] == "st" and e[2:] == (2, 0, 0):
                    load_group(e[1], 3)
            for k in range(4):
                sp.wait_ge(s_out[k], 16 * B * TT // 4)

        @block.tensor
        def _(pe):
            def mod():
                pe.wait_ge(s_dve0, 1)
                pe.wait_ge(s_ada, 48)
                bank_ = wait_bank(pe, ("mod",))
                chunks = [(wada, sc, m) for m in (0, 1, 2, 3, 6, 7, 8, 9)] + [(wg, cs, 0), (wg, cs, 1), (wb, cs, 0), (wb, cs, 1)]
                for n, (w, v, m) in enumerate(chunks):
                    for k in range(CC):
                        mm = pe.matmul(bank_[:, n * B:(n + 1) * B], w[:, k, m * P:(m + 1) * P], v[:, k, :],
                                       start=(k == 0), stop=(k == CC - 1))
                mm.then_inc(job_full, 1)

            def rows_(b, n):
                bank_ = wait_bank(pe, ("rows", b, n))
                w, v = ((wada[:, :, 2 * C:3 * C], scB), (wada[:, :, 5 * C:6 * C], scB), (wg, cB), (wb, cB))[n]
                for k in range(CC):
                    mm = pe.matmul(bank_[:, 0:C], v[:, k, b, :], w[:, k, :], start=(k == 0), stop=(k == CC - 1))
                mm.then_inc(job_full, 1)

            def lnT(e):
                _, u, k, th, cc = e
                bank_ = wait_bank(pe, e)
                pe.wait_ge(xn_done, 4 * counts[("xn", u, k, th)])
                for t in range(4):
                    mm = pe.transpose(bank_[:, t * P:(t + 1) * P], xn[:, t, cc * P:(cc + 1) * P], idf[:, :])
                mm.then_inc(job_full, 1)

            def qk(e):
                _, u, j = e
                side, cc, th = j // 4, j // 2 % 2, j % 2
                bank_ = wait_bank(pe, e)
                pe.wait_ge(s_w[f"qkv{u // B}"], 16)
                job_taken(pe, ("lnT", u, 0, th, CC - 1))
                for k in range(CC):
                    mm = pe.matmul(bank_[:, :], wqkv[u // B][:, k, side * C + cc * P:side * C + (cc + 1) * P],
                                   hT[:, k, th * 512:(th + 1) * 512], start=(k == 0), stop=(k == CC - 1))
                mm.then_inc(job_full, 1)

            def v(e):
                _, u, t = e
                bank_ = wait_bank(pe, e)
                for k in range(CC):
                    mm = pe.matmul(bank_[:, 0:C], hT[:, k, t * P:(t + 1) * P], wqkv[u // B][:, k, 2 * C:3 * C],
                                   start=(k == 0), stop=(k == CC - 1))
                mm.then_inc(job_full, 1)

            def smax(e):
                _, u, i, m = e
                n = counts[e]
                h, qt, kh = m // 8, m // 2 % 4, m % 2
                s, q0 = slot(u, i // 2), (i % 2) * QW + qt * P
                if m == 0:
                    pe.wait_ge(loaded[s], 16 * LOADS * loads(u, i // 2))
                if n > 2:
                    pe.wait_ge(mx_out, n - 2)
                pe.matmul(M[(n - 1) % 2][:, :], qs[s][0:ROW_MAX, h, q0:q0 + P], ks[s][0:ROW_MAX, h, kh * 512:(kh + 1) * 512],
                          start=True, stop=True).then_inc(mx_full, 1)

            def mrow_(e):
                bank_ = wait_bank(pe, e)
                k = item(e[1], e[2]) % 2
                pe.wait_ge(mpart_done, item(e[1], e[2]) + 1)
                for t in range(TQ):
                    mm = pe.matmul(bank_[0:3 * HG, t * P:(t + 1) * P],
                                   mpart[:, k, :, :].rearrange("p r (h t) -> p (r h) t", t=TQ)[:, :, t], idb[:, :],
                                   start=True, stop=True)
                mm.then_inc(job_full, 1)

            def st(e):
                _, u, i, s, h = e
                n = counts[e]
                sl, q0 = slot(u, i // 2), (i % 2) * QW
                if s == 0 and h == 0:
                    k = item(u, i)
                    pe.wait_ge(mrow_in[k % 2], 48 * (k // 2 + 1))
                if n > 3:
                    pe.wait_ge(exp_done, n - 3)
                pe.matmul(A[(n - 1) % 3][:, :], ks[sl][0:ROWS, h, s * P:(s + 1) * P], qs[sl][0:ROWS, h, q0:q0 + QW],
                          start=True, stop=True).then_inc(st_full, 1)

            def pv(e):
                _, u, i, s = e
                n = counts[e]
                pe.wait_ge(exp_done, HG * n)
                if s == 0:
                    if item(u, i) > 0:
                        pe.wait_ge(acc_out, item(u, i))
                    else:
                        pe.wait_ge(s_acc, 1)
                    if i == 0:
                        job_taken(pe, ("v", u, TT - 1))
                for h in range(HG):
                    mm = pe.matmul(acc[h * CW:h * CW + VW, :], va[:, s, (i // 2) * HG + h, :], prob[:, (n - 1) % 2, h, :],
                                   start=(s == 0), stop=(s == KT - 1), skip_group_check=True)
                mm.then_inc(pv_done, 1)

            def oT_(e):
                bank_ = wait_bank(pe, e)
                n = item(e[1], e[2])
                pe.wait_ge(acc_out, n + 1)
                for t in range(TQ):
                    mm = pe.transpose(bank_[:, t * P:(t + 1) * P], oraw[:, n % 2, t * P:(t + 1) * P], idf[:, :])
                mm.then_inc(job_full, 1)

            def opT(e):
                _, u, th, cc = e
                bank_ = wait_bank(pe, e)
                job_taken(pe, ("oT", u, ITEMS - 1))
                for t in range(4):
                    mm = pe.transpose(bank_[:, t * P:(t + 1) * P], otok[:, 4 * th + t, cc * P:(cc + 1) * P], idf[:, :])
                mm.then_inc(job_full, 1)

            def proj(e):
                _, u, t = e
                bank_ = wait_bank(pe, e)
                pe.wait_ge(s_w[f"proj{u // B}"], 16)
                job_taken(pe, ("opT", u, t // 4, CC - 1))
                for k in range(CC):
                    mm = pe.matmul(bank_[:, 0:C], oT[:, k, t * P:(t + 1) * P], wproj[u // B][:, k, :],
                                   start=(k == 0), stop=(k == CC - 1))
                mm.then_inc(job_full, 1)

            def fc1(e):
                _, u, tb, f2 = e
                bank_ = wait_bank(pe, e)
                pe.wait_ge(s_w["fc1"], 16)
                job_taken(pe, ("lnT", u, 1, tb // 2, CC - 1))
                for f in range(2):
                    for k in range(CC):
                        c0 = (2 * f2 + f) * P
                        mm = pe.matmul(bank_[:, f * BW:(f + 1) * BW], wfc1[:, k, c0:c0 + P], hT[:, k, tb * BW:(tb + 1) * BW],
                                       start=(k == 0), stop=(k == CC - 1))
                mm.then_inc(job_full, 1)

            def fc2(e):
                _, u, tb, t = e
                bank_ = wait_bank(pe, e)
                pe.wait_ge(s_w["fc2"], 16)
                job_taken(pe, ("fc1", u, tb, FC // 2 - 1))
                for f in range(FC):
                    mm = pe.matmul(bank_[:, 0:C], ge[:, f, t * P:(t + 1) * P], wfc2[:, f, :], start=(f == 0), stop=(f == FC - 1))
                mm.then_inc(job_full, 1)

            pe.wait_ge(s_id, 2)
            does = dict(lnT=lnT, qk=qk, v=v, smax=smax, mrow=mrow_, st=st, pv=pv, oT=oT_, opT=opT, proj=proj, fc1=fc1, fc2=fc2)
            for e in plan:
                if e[0] == "mod":
                    mod()
                elif e[0] == "rows":
                    rows_(e[1], e[2])
                elif e[0] in does:
                    does[e[0]](e)

        @block.scalar
        def _(act):
            act.dma_start(cs[:, :, :], cT.rearrange("(k p) b -> p k b", p=P)).then_inc(s_small, 16)
            act.dma_start(col[:, :], cols).then_inc(s_small, 16)
            act.dma_start(row[:, :, :], rows.rearrange("(o r) c -> o r c", o=1).to_broadcast([P, len(ROWV), C])).then_inc(s_small, 16)
            act.dma_start(mk8, mask).then_inc(s_small, 16)
            act.dma_start(m8, mask.rearrange("(o b) n -> o b n", o=1).to_broadcast([P, B, N])).then_inc(s_small, 16)
            act.wait_ge(s_small, 80)
            act.activation(sig[:, 0, :, :], cs[:, :, :], ACT.Exp, scale=-1.0).then_inc(s_act0, 1)

            def lnT(e):
                _, u, k, th, cc = e
                if u == 0 and k == 0:
                    act.wait_ge(s_modc, 1)
                if u < B:
                    a, b_ = modc[:, 4 * k + 2 + cc, u % B:u % B + 1], modc[:, 4 * k + cc, u % B:u % B + 1]
                else:
                    a, b_ = l1c[:, cc, u % B:u % B + 1], l1c[:, 2 + cc, u % B:u % B + 1]
                bank_ = job_ready(act, e)
                act.activation(hT[:, cc, th * 512:(th + 1) * 512], bank_[:, :], ACT.Identity, bias=b_, scale=a).then_inc(job_act, 1)

            def qk(e):
                _, u, j = e
                n = counts[e]
                side, cc = j // 4, j // 2 % 2
                c0 = COLS[f"qk{u // B}"] + 2 * side + cc
                bank_ = job_ready(act, e)
                if n > 2:
                    act.wait_ge(parts_done, n - 2)
                act.activation(qf[:, (n - 1) % 2, :], bank_[:, :], ACT.Identity, bias=col[:, c0:c0 + 1]).then_inc(job_act, 1)

            def mrow_(e):
                k = item(e[1], e[2])
                bank_ = job_ready(act, e)
                if k >= 2:
                    act.wait_ge(mrow_in[k % 2], 48 * (k // 2))
                act.activation(mrow[:, k % 2, :], bank_[0:3 * HG, :], ACT.Identity).then_inc(job_act, 1)

            def st(e):
                _, u, i, s, h = e
                n = counts[e]
                step = (n - 1) // HG
                act.wait_ge(st_full, n)
                if step >= 2:
                    act.wait_ge(pv_done, step - 1)
                act.activation(prob[:, step % 2, h, :], A[(n - 1) % 3][:, :], ACT.Exp).then_inc(exp_done, 1)

            def evac(e):
                n = item(e[1], e[2])
                act.wait_ge(pv_done, KT * (n + 1))
                if n >= 2:
                    job_taken(act, ("oT", *divmod(n - 2, ITEMS)))
                act.activation(oraw[:, n % 2, :], acc[:, :], ACT.Identity).then_inc(acc_out, 1)

            def opT(e):
                _, u, th, cc = e
                bank_ = job_ready(act, e)
                act.activation(oT[:, cc, th * 512:(th + 1) * 512], bank_[:, :], ACT.Identity).then_inc(job_act, 1)

            def fc1(e):
                _, u, tb, f2 = e
                bank_ = job_ready(act, e)
                if u == 0 and tb == 0 and f2 == 0:
                    act.wait_ge(s_rows, 1)
                if tb > 0:
                    act.wait_ge(job_full, jobs[("fc2", u, tb - 1, 1)][0] + 1)
                c0 = COLS["fc1"] + 2 * f2
                act.activation(ge[:, 2 * f2, :], bank_[:, 0:BW], ACT.Gelu_apprx_tanh, bias=col[:, c0:c0 + 1])
                act.activation(ge[:, 2 * f2 + 1, :], bank_[:, BW:2 * BW], ACT.Gelu_apprx_tanh, bias=col[:, c0 + 1:c0 + 2]).then_inc(job_act, 1)

            does = dict(lnT=lnT, mrow=mrow_, st=st, evac=evac, opT=opT, fc1=fc1)
            for e in plan:
                if e[0] in does:
                    does[e[0]](e)
                elif e[0] == "qk" and taker(e) == "act":
                    qk(e)

        @block.vector
        def _(dve):
            own = [0]

            def link(ins):
                own[0] += 1
                ins.then_inc(dve_self, 1)
                dve.wait_ge(dve_self, own[0])

            R = {n: row[:, k, :] for k, n in enumerate(ROWV)}
            dve.wait_ge(s_act0, 1)
            link(dve.tensor_scalar(sig[:, 1, :, :], sig[:, 0, :, :], 1.0, None, ALU.add))
            link(dve.reciprocal(sig[:, 0, :, :], sig[:, 1, :, :]))
            link(dve.tensor_tensor(sc[:, :, :], cs[:, :, :], sig[:, 0, :, :], ALU.mult))
            dve.tensor_copy(scB, sc[:, :, :].rearrange("p k (b o) -> p k b o", o=1).to_broadcast([P, CC, B, P]))
            dve.tensor_copy(cB, cs[:, :, :].rearrange("p k (b o) -> p k b o", o=1).to_broadcast([P, CC, B, P])).then_inc(s_dve0, 1)
            dve.memset(acc[:, :], 0.0).then_inc(s_acc, 1)
            link(dve.memset(mk[:, 0, :], 1.0))
            link(dve.memset(mk[:, 1, :], 0.0))
            dve.tensor_copy(mk[0:B, 0, :], mk8)
            dve.tensor_scalar(mk[0:B, 1, :], mk8, -1.0, -MASKED, ALU.add, ALU.mult).then_inc(s_mask, 1)
            link(dve.tensor_scalar(vq[:, :, :], m8, float(HD) ** -0.5, None, ALU.mult))

            def mod():
                bank_ = job_ready(dve, ("mod",))
                bias = col[:, COLS["mod"]:COLS["mod"] + 12].rearrange("p (n o) -> p n o", o=1).to_broadcast([P, 12, B])
                own[0] += 0
                dve.tensor_tensor(modc[:, :, :], bank_[:, 0:12 * B].rearrange("p (n b) -> p n b", b=B), bias, ALU.add).then_inc(job_dve, 1)
                dve.wait_ge(job_dve, jobs[("mod",)][2])
                link(dve.tensor_scalar(modc[:, 2:4, :], modc[:, 2:4, :], 1.0, None, ALU.add))
                link(dve.tensor_scalar(modc[:, 6:8, :], modc[:, 6:8, :], 1.0, None, ALU.add))
                for cc in range(CC):
                    g, b_ = (col[:, COLS[n] + cc:COLS[n] + cc + 1] for n in ("lng", "lnb"))
                    dve.tensor_scalar(l1c[:, cc, :], modc[:, 8 + cc, :], g, None, ALU.mult)
                    link(dve.tensor_scalar(l1c[:, 2 + cc, :], modc[:, 8 + cc, :], b_, None, ALU.mult))
                dve.tensor_tensor(l1c[:, 2:4, :], l1c[:, 2:4, :], modc[:, 10:12, :], ALU.add).then_inc(s_modc, 1)

            def rows_(b, n):
                e = ("rows", b, n)
                bank_ = job_ready(dve, e)
                name = ("gate_msa", "gate_mlp", "gamma", "beta")[n]
                dve.tensor_tensor(gate[:, b, n, :], bank_[:, 0:C], R[name], ALU.add).then_inc(job_dve, 1)
                dve.wait_ge(job_dve, jobs[e][2])
                if n < 2:
                    link(dve.tensor_tensor(gbias[:, b, n, :], gate[:, b, n, :], R[("proj0", "fc2")[n]], ALU.mult))
                if n == 3:
                    link(dve.tensor_tensor(tmp[:, 0, :], gate[:, b, 2, :], R["ln_b"], ALU.mult))
                    link(dve.tensor_tensor(gate[:, b, 3, :], gate[:, b, 3, :], tmp[:, 0, :], ALU.add))
                    i = dve.tensor_tensor(gate[:, b, 2, :], gate[:, b, 2, :], R["ln_g"], ALU.mult)
                    link(i)
                    if b == B - 1:
                        dve.memset(rec[:, :, :, :], 0.0).then_inc(s_rows, 1)

            def stats(e):
                _, u, k = e
                b = u % B
                if k == 0 and u < B:
                    dve.wait_ge(s_x[b], 16)
                if k == 1 or u >= B:
                    pass
                for t in range(TT):
                    i = dve.bn_stats(stat[:, t, :], xs[:, b * TT + t, :])
                link(i)
                for t in range(TT):
                    i = dve.bn_aggr(mv[:, t, :], stat[:, t, :])
                i.then_inc(stats_done, 1)
                dve.wait_ge(stats_done, counts[e])

            def xn_(e):
                _, u, k, th = e
                dve.wait_ge(rstd_done, counts[("stats", u, k)])
                n = counts[e]
                if th == 1:
                    dve.wait_ge(job_full, jobs[("lnT", u, k, 0, CC - 1)][0] + 1)
                elif n > 2:
                    prev = [p for p in plan[:plan.index(e)] if p[0] == "lnT"][-1]
                    dve.wait_ge(job_full, jobs[prev][0] + 1)
                if th == 0 and (before := sum(p[0] == "fin" for p in plan[:plan.index(e)])):
                    for k4 in range(4):
                        dve.wait_ge(s_out[k4], 16 * before // 4)
                for t in range(4):
                    tt = 4 * th + t
                    dve.tensor_scalar(xn[:, t, :], xs[:, (u % B) * TT + tt, :], mv[:, tt, 0:1], rstd[:, 1, tt:tt + 1],
                                      ALU.subtract, ALU.mult).then_inc(xn_done, 1)

            def qk(e):
                _, u, j = e
                n = counts[e]
                cc, th = j // 2 % 2, j % 2
                c0 = COLS["qk0"] + cc
                bank_ = job_ready(dve, e)
                if n > 2:
                    dve.wait_ge(parts_done, n - 2)
                dve.scalar_tensor_tensor(out=qf[:, (n - 1) % 2, :], in0=bank_[:, :], scalar=col[:, c0:c0 + 1],
                                         in1=vq[:, u, th * 512:(th + 1) * 512], op0=ALU.add, op1=ALU.mult).then_inc(job_dve, 1)

            def v(e):
                _, u, t = e
                bank_ = job_ready(dve, e)
                if u > 0 and t == 0:
                    dve.wait_ge(pv_done, counts[("pv", u - 1, ITEMS - 1, KT - 1)])
                dve.tensor_tensor(va[:, t, :, 0:HD], bank_[:, 0:C].rearrange("p (h d) -> p h d", h=H),
                                  R[f"v{u // B}"].rearrange("p (h d) -> p h d", h=H), ALU.add).then_inc(job_dve, 1)

            def smax(e):
                _, u, i, m = e
                n = counts[e]
                dve.wait_ge(mx_full, n)
                dve.tensor_reduce(mx[:, item(u, i) % 2, m // 2, m % 2:m % 2 + 1], M[(n - 1) % 2][:, :], AX.X, ALU.max).then_inc(mx_out, 1)

            def neg(e):
                k = item(e[1], e[2])
                dve.wait_ge(mx_out, counts[("smax", e[1], e[2], 31)])
                if k >= 2:
                    dve.wait_ge(mpart_done, k - 1)
                dve.tensor_reduce(negm[:, k % 2, :], mx[:, k % 2, :, :], AX.X, ALU.max, negate=True).then_inc(neg_done, 1)
                dve.wait_ge(neg_done, k + 1)

            def oT_(e):
                _, u, i = e
                k = item(u, i)
                bank_ = job_ready(dve, e)
                o = bank_[:, :].rearrange("p (t h w) -> p t h w", t=TQ, w=CW)
                r = rec[:, k % 2, :, :]
                link(dve.reciprocal(r, o[:, :, :, HD]))
                if u >= B:
                    link(dve.tensor_scalar(r, r, float(C) ** -0.5, None, ALU.mult))
                g, qh = i // 2, i % 2
                if i < 2 and u > 0:
                    dve.wait_ge(job_full, jobs[("opT", u - 1, 1, CC - 1)][0] + 1)
                dst = otok[:, qh * TQ:(qh + 1) * TQ, g * HG * HD:(g + 1) * HG * HD].rearrange("p t (h d) -> p t h d", h=HG)
                dve.tensor_tensor(dst, o[:, :, :, 0:HD], r.rearrange("p t (h o) -> p t h o", o=1).to_broadcast([P, TQ, HG, HD]),
                                  ALU.mult).then_inc(job_dve, 1)

            def residual(e, t, k):
                u = e[1]
                bank_ = job_ready(dve, e)
                xt = xs[:, (u % B) * TT + t, :]
                if k == 0 or t == 0:
                    dve.wait_ge(biased, counts[("bias_in", u, k)])
                if u < B:
                    link(dve.tensor_tensor(tmp[:, t % 2, :], bank_[:, 0:C], gate[:, u % B, k, :], ALU.mult))
                    dve.tensor_tensor(xt, tmp[:, t % 2, :], xt, ALU.add).then_inc(job_dve, 1)
                else:
                    dve.tensor_tensor(xt, bank_[:, 0:C], xt, ALU.add).then_inc(job_dve, 1)
                if t == TT - 1:
                    dve.wait_ge(job_dve, jobs[e][2])

            def fin(e):
                _, u, t = e
                b = u % B
                k = t % 4
                n = counts[e]
                if t == 0:
                    dve.wait_ge(rstd_done, counts[("stats", u, 1)])
                if n > 4:
                    dve.wait_ge(s_out[k], 16 * ((n - 1) // 4))
                    dve.wait_ge(fin_x, n - 4)
                link(dve.tensor_scalar(xn[:, k, :], xs[:, b * TT + t, :], mv[:, t, 0:1], rstd[:, 1, t:t + 1], ALU.subtract, ALU.mult))
                link(dve.tensor_tensor(xn[:, k, :], xn[:, k, :], gate[:, b, 2, :], ALU.mult))
                link(dve.tensor_tensor(xn[:, k, :], xn[:, k, :], gate[:, b, 3, :], ALU.add))
                dve.tensor_tensor(xn[:, k, :], xn[:, k, :], xs[:, b * TT + t, :], ALU.add).then_inc(fin_x, 1)

            does = dict(stats=stats, xn=xn_, v=v, smax=smax, neg=neg, oT=oT_, fin=fin)
            for e in plan:
                if e[0] == "mod":
                    mod()
                elif e[0] == "rows":
                    rows_(e[1], e[2])
                elif e[0] == "proj":
                    residual(e, e[2], 0)
                elif e[0] == "fc2":
                    residual(e, 2 * e[2] + e[3], 1)
                elif e[0] == "qk" and taker(e) == "dve":
                    qk(e)
                elif e[0] in does:
                    does[e[0]](e)

        @block.gpsimd
        def _(pool):
            own = [0]

            def link(ins):
                own[0] += 1
                ins.then_inc(pool_self, 1)
                pool.wait_ge(pool_self, own[0])

            link(pool.memset(idf[:, :], 0.0))
            pool.affine_select(out=idf[:, :], in_=idf[:, :], compare_op=ALU.not_equal, fill=1.0, base=0,
                               pattern=[[-1, P]], channel_multiplier=1).then_inc(s_id, 1)
            pool.wait_ge(s_id, 1)
            pool.tensor_copy(idb[:, :], idf[:, :]).then_inc(s_id, 1)
            pool.wait_ge(s_id, 2)
            for s in range(SLOTS):
                pool.memset(ks[s][ROW_MASK:ROWS, :, :], 1.0).then_inc(s_ones, 1)
                pool.wait_ge(s_ones, s + 1)
            pool.memset(power[:, :], -0.5).then_inc(s_const, 1)
            link(pool.memset(va[:, :, :, HD:VW], 1.0))

            def stats(e):
                _, u, k = e
                pool.wait_ge(stats_done, counts[e])
                pool.wait_ge(s_const, 1)
                if counts[e] > 1:
                    prev = [p for p in plan[:plan.index(e)] if p[0] in ("xn", "fin")][-1]
                    if prev[0] == "xn":
                        pool.wait_ge(xn_done, 4 * counts[prev])
                    else:
                        pool.wait_ge(fin_x, counts[prev])
                link(pool.tensor_scalar(rstd[:, 0, :], mv[:, :, 1], EPS[u // B], 1.0, ALU.add, ALU.mult))
                pool.tensor_tensor(rstd[:, 1, :], rstd[:, 0, :], power[:, :], ALU.pow).then_inc(rstd_done, 1)

            def qk(e):
                n = counts[e]
                k = (n - 1) % 2
                job_taken(pool, e)
                if n > 2:
                    pool.wait_ge(stored[k], 16 * ((n - 1) // 2))
                f = qf[:, k, :]
                link(pool.tensor_scalar(parts[:, k, 0, :], f, 1.0, 0.0, ALU.mult, ALU.add))
                link(pool.tensor_tensor(f, f, parts[:, k, 0, :], ALU.subtract))
                link(pool.tensor_scalar(parts[:, k, 1, :], f, 1.0, 0.0, ALU.mult, ALU.add))
                pool.tensor_tensor(parts[:, k, 2, :], f, parts[:, k, 1, :], ALU.subtract).then_inc(parts_done, 1)

            def neg(e):
                n = item(e[1], e[2])
                k = n % 2
                pool.wait_ge(neg_done, n + 1)
                if n >= 2:
                    pool.wait_ge(job_full, jobs[("mrow", *divmod(n - 2, ITEMS))][0] + 1)
                f = negm[:, k, :]
                link(pool.tensor_scalar(mpart[:, k, 0, :], f, 1.0, 0.0, ALU.mult, ALU.add))
                link(pool.tensor_tensor(f, f, mpart[:, k, 0, :], ALU.subtract))
                link(pool.tensor_scalar(mpart[:, k, 1, :], f, 1.0, 0.0, ALU.mult, ALU.add))
                pool.tensor_tensor(mpart[:, k, 2, :], f, mpart[:, k, 1, :], ALU.subtract).then_inc(mpart_done, 1)

            def bias_in(e):
                _, u, k = e
                pool.wait_ge(xn_done, 4 * counts[("xn", u, k, 1)])
                if u == 0 and k == 0:
                    pool.wait_ge(s_rows, 1)
                bias = gbias[:, u % B, k, :] if u < B else row[:, ROWV.index("proj1"), :]
                for t in range(TT):
                    xt = xs[:, (u % B) * TT + t, :]
                    i = pool.tensor_tensor(xt, xt, bias, ALU.add)
                i.then_inc(biased, 1)

            does = dict(stats=stats, qk=qk, neg=neg, bias_in=bias_in)
            for e in plan:
                if e[0] in does:
                    does[e[0]](e)


def kernel(**inputs):
    import numpy as np
    import concourse.bacc as bacc
    from concourse.bass_utils import run_bass_kernel_spmd

    a = {n: np.asarray(v) for n, v in inputs.items()}

    def t(w):
        return np.ascontiguousarray(w.T)

    def chunks(v):
        return v.reshape(-1, P).T

    w1 = a["L1_cond_Wqkv"].reshape(C, 3, C).transpose(1, 0, 2).reshape(3 * C, C)
    b1 = a["L1_cond_bqkv"].reshape(C, 3).T.reshape(3 * C)
    b0, ada = a["L0_cond_qkv_b"], a["L0_cond_ada_b"].reshape(6, C)
    cols = np.concatenate([
        chunks(b0[:2 * C]), chunks(b1[:2 * C]), chunks(a["L0_cond_fc1_b"]),
        chunks(ada[0]), chunks(ada[1]), chunks(ada[3]), chunks(ada[4]), chunks(a["L1_cond_bg"]), chunks(a["L1_cond_bb"]),
        chunks(a["L1_cond_ln_g"]), chunks(a["L1_cond_ln_b"])], axis=1)
    rows = np.stack([b0[2 * C:], b1[2 * C:], a["L0_cond_proj_b"], a["L1_cond_bp"], a["L0_cond_fc2_b"], ada[2], ada[5],
                     a["L1_cond_bg"], a["L1_cond_bb"], a["L1_cond_ln_g"], a["L1_cond_ln_b"]])
    arrays = {
        "x": a["x"], "cT": t(a["cond_1024"]), "mask": a["mask_BxS_bk1"],
        "adaT": t(a["L0_cond_ada_w"]), "WgT": t(a["L1_cond_Wg"]), "WbT": t(a["L1_cond_Wb"]),
        "qkvT0": t(a["L0_cond_qkv_w"]), "qkvT1": t(w1), "projT0": t(a["L0_cond_proj_w"]), "projT1": t(a["L1_cond_Wp"]),
        "fc1T": t(a["L0_cond_fc1_w"]), "fc2T": t(a["L0_cond_fc2_w"]), "cols": cols, "rows": rows,
    }
    arrays = {f"in_{n}": np.ascontiguousarray(v) for n, v in arrays.items()}
    nc = bacc.Bacc("TRN2", target_bir_lowering=False, num_devices=1)
    args = [nc.dram_tensor(n, v.shape, mybir.dt.from_np(v.dtype), kind="ExternalInput").ap() for n, v in arrays.items()]
    args.append(nc.dram_tensor("out_0", (B, N, C), F32, kind="ExternalOutput").ap())
    build(nc, *args)
    r = run_bass_kernel_spmd(nc, [arrays], core_ids=[0])
    return r.results[0]["out_0"]
```

```python
import math
from contextlib import ExitStack

import concourse.bass as bass
from concourse import mybir

ALU = mybir.AluOpType
ACT = mybir.ActivationFunctionType
AX = mybir.AxisListType
F32 = mybir.dt.float32
BF16 = mybir.dt.bfloat16
U8 = mybir.dt.uint8

P = 128
B, N, C = 2, 1024, 256
H, HD = 16, 16
MLP = 4 * C
TT = N // P
CC = C // P
HG = 4
GROUPS = H // HG
QW = 512
QH = N // QW
TQ = QW // P
KT = N // P
ITEMS = GROUPS * QH
STEPS = ITEMS * KT
FC = MLP // P
TB = 4
BW = N // TB
LAYERS = 2
UNITS = LAYERS * B
EPS = (1e-6, 1e-5)
GELU_SCALE = (2.0 / math.pi) ** 0.5
GELU_CUBE = 0.044715
MASKED = -float(2 ** 30)
BLOCKS = (3, 2, 1)
ROW_MASK = sum(BLOCKS) * HD
ROW_MAX = ROW_MASK + 1
ROWS = ROW_MAX + 3
BANKS = 7
LAG = 2
LEAD = 12
VW = HD + 1
CW = 32
SLOTS = 3

COLS = dict(qk0=0, qk1=4, fc1=8, mod=16, lng=28, lnb=30)
NCOLS = 32
ROWV = ("v0", "v1", "proj0", "proj1", "fc2", "gate_msa", "gate_mlp", "gamma", "beta", "ln_g", "ln_b")


def schedule():
    plan = []

    def norm(u, k):
        return [[("stats", u, k, th)] for th in range(2)] + [
            x for th in range(2) for x in ([("xn", u, k, th)], [("lnT", u, k, th, cc) for cc in range(CC)])]

    def qk(u, j):
        return [("qk", u, j), ("qk", u, j + 4)]

    def after(u):
        def half(th):
            return [[("opT", u, th, cc) for cc in range(CC)]] + pairs("proj", th)

        def pairs(kind, th):
            return [[(kind, u, t), (kind, u, t + 1)] for t in (4 * th, 4 * th + 2)]
        if u >= B:
            steps = [x for th in range(2) for x in (*half(th), [("stats", u, 1, th)], *pairs("fin", th))]
            return steps if u == UNITS - 1 else [[e] for x in steps for e in x]
        stats0, stats1, xn0, lnT0, xn1, lnT1 = norm(u, 1)
        a0, a1 = half(0), half(1)
        steps = [*a0, stats0 + a1[0], a1[1], xn0 + a1[2], lnT0 + [("bias_in", u, 1, 0)] + stats1]
        for tb in range(TB):
            f = [("fc1", u, tb, k) for k in range(4)]
            g = [("tanh", u, tb, k) for k in range(4)]
            o = [("gelu", u, tb, k) for k in range(4)]
            steps += [[f[0]], [g[0], f[1]], [o[0], g[1]], [f[2], o[1]], [g[2], f[3]], [o[2], g[3]], [o[3]],
                      [("fc2", u, tb, 0), ("fc2", u, tb, 1)]]
        n = len(steps) - 8 * TB
        steps[n + 1] += xn1 + [("bias_in", u, 1, 1)]
        steps[n + 2] += lnT1
        return steps

    def maxima(step, k):
        u, i, m = step // STEPS, step // KT % ITEMS, 4 * (step % KT) + k
        if u >= UNITS:
            return []
        return [("smax", u, i, m)] + ([("neg", u, i)] if m == 4 * KT - 1 else [])

    def max_rows(step):
        u, i = step // STEPS, step // KT % ITEMS
        return [("mrow", u, i)] if step % KT == KT - 1 and 0 <= u < UNITS else []

    stats0, stats1, xn0, lnT0, xn1, lnT1 = norm(0, 0)
    plan += [*stats0, ("silu",), *stats1, *xn0, ("mod", 0), *lnT0, ("quarter",), *xn1, *qk(0, 0)]
    plan += [*lnT1, ("qk", 0, 1), ("mask",), ("qk", 0, 5), ("load", 0, 0)]
    stats0, stats1, xn0, lnT0, xn1, lnT1 = norm(1, 0)
    plan += [*qk(0, 2), *stats0, *[("v", 0, t) for t in range(4)], *stats1, *qk(0, 3), *[("v", 0, t) for t in range(4, TT)]]
    plan += [*xn0, ("load", 0, 1), ("load", 0, 2)]
    side = [lnT0, xn1, [("qk", 1, 0)], lnT1, [("qk", 1, 4)], [("mod", 1)]]
    rows = [[("rows", b, k)] for b in range(B) for k in range(2)]
    for j in (1, 5, 2, 6, 3, 7):
        side += [[("qk", 1, j)], rows.pop(0) if rows else []]
    for step in range(LEAD):
        for k in range(4):
            plan += maxima(step, k)
            if k % 2:
                plan += side.pop(0) if side else []
        plan += max_rows(step - LAG)
    for steps in side:
        plan += steps
    for u in range(UNITS):
        last = u == UNITS - 1
        side = [[], []] + (after(u - 1) if u > 0 else [])
        if u == 0:
            side += [[("rows", b, k)] for b in range(B) for k in (2, 3)]
            side += [[("bias_in", b, 0, th)] for b in range(B) for th in range(2)]
        if 0 < u < UNITS - 1:
            stats0, stats1, xn0, lnT0, xn1, lnT1 = norm(u + 1, 0)
            side[-5] += stats0
            side[-3] += xn0
            side[-2] += lnT0
            side += [stats1 + qk(u + 1, 0), xn1, lnT1, qk(u + 1, 1), [], qk(u + 1, 2), [], qk(u + 1, 3)]
            side += [[("bias_in", u + 1, 0, th)] for th in range(2)]
        if last:
            end = after(u)
            side += [[]] * (7 * KT + 2 - len(side)) + end[:6]
        for i in range(ITEMS):
            for s in range(KT):
                step = u * STEPS + i * KT + s + LEAD
                extra = list(side.pop(0)) if side else []
                if i == ITEMS - 1 and s > 0 and not last:
                    extra.append(("v", u + 1, s - 1))
                if i == 0 and s == 0 and u > 0:
                    extra.append(("v", u, KT - 1))
                if s == 1 and u * ITEMS + i > 0:
                    extra.append(("oT", *divmod(u * ITEMS + i - 1, ITEMS)))
                extra += max_rows(step - LAG)
                st = [("st", u, i, s, k) for k in range(4)]
                sm = [maxima(step, k) for k in range(4)]
                plan += [st[0], *sm[0], st[1], *sm[1], st[2], *sm[2], st[3], *sm[3], *extra]
                if u + i + s > 0:
                    n = u * STEPS + i * KT + s - 1
                    pu, pi, ps = n // STEPS, n // KT % ITEMS, n % KT
                    plan.append(("pv", pu, pi, ps))
                    if ps == KT - 1:
                        plan.append(("evac", pu, pi))
                if (u, i, s) == (0, 0, 4):
                    plan.append(("weights",))
                if (i, s) == (0, 1) and u > 0:
                    plan.append(("load", u, 2))
                if (i, s) == (2, 1):
                    plan.append(("load", u, 3))
                if (i, s) == (5, 6) and not last:
                    plan.append(("load", u + 1, 0))
                if (i, s) == (6, 1) and not last:
                    plan.append(("load", u + 1, 1))
        assert not side, len(side)
    plan += [("pv", u, ITEMS - 1, KT - 1), ("evac", u, ITEMS - 1), ("oT", u, ITEMS - 1)]
    for steps in end[6:]:
        plan += steps
    return plan


def taker(e):
    kind = e[0]
    if kind in ("mod", "rows", "v", "oT", "proj", "fc2"):
        return "dve"
    if kind == "qk":
        return "dve" if e[1] // B == 0 and e[2] < 4 else "act"
    if kind in ("lnT", "mrow", "opT", "fc1"):
        return "act"
    return None


def splitter(e):
    return "dve" if e[1:] in ((0, 4), (0, 5)) else "pool"


def build(nc, x, cT, mask, adaT, WgT, WbT, qkvT0, qkvT1, projT0, projT1, fc1T, fc2T, cols, rows, out):
    plan = schedule()
    jobs, taken = {}, {"dve": 0, "act": 0}
    fills = [e for e in plan if taker(e) is not None or e[0] in ("st", "smax")]
    turn = {e: n for n, e in enumerate(fills)}
    for e in plan:
        if (w := taker(e)) is not None:
            taken[w] += 1
            jobs[e] = (len(jobs), w, taken[w])

    counts = {}
    seen = {}
    for e in plan:
        seen[e[0]] = seen.get(e[0], 0) + 1
        counts[e] = seen[e[0]]

    scratch = nc.dram_tensor("qk_parts", (2, 2, 3, C, N), BF16, kind="Internal").ap()

    mask_rows = nc.dram_tensor("mask_rows", (3, 2, N), BF16, kind="Internal").ap()

    with ExitStack() as ctx:
        def sb(name, shape, dt=F32):
            return ctx.enter_context(nc.sbuf_tensor(name, shape, dt))

        def bank(name):
            return ctx.enter_context(nc.psum_tensor(name, [P, 512], F32))

        def sem(name):
            return ctx.enter_context(nc.semaphore(name))

        xs = sb("xs", [P, B * TT, C])
        xn = sb("xn", [P, 4, C])
        stat = sb("stat", [P, TT, 6])
        mv = sb("mv", [P, TT, 2])
        rstd = sb("rstd", [P, 2, TT])
        power = sb("power", [P, TT])
        hT = sb("hT", [P, CC, N])
        qf = sb("qf", [P, 2, 512])
        parts = sb("parts", [P, 2, 3, 512], BF16)
        qs = [sb(f"qs{i}", [P, HG, N], BF16) for i in range(SLOTS)]
        ks = [sb(f"ks{i}", [P, HG, N], BF16) for i in range(SLOTS)]
        va = sb("va", [P, KT, H, VW])
        prob = sb("prob", [P, 2, HG, QW])
        mx = sb("mx", [P, 2, HG * TQ, 2])
        negm = sb("negm", [P, 2, HG * TQ])
        mpart = sb("mpart", [P, 2, 3, HG * TQ], BF16)
        mrow = sb("mrow", [3 * HG, 2, QW], BF16)
        oraw = sb("oraw", [P, 2, QW])
        rec = sb("rec", [P, 2, TQ, HG])
        otok = sb("otok", [P, TT, C])
        oT = sb("oT", [P, CC, N])
        tmp = sb("tmp", [P, 2, C])
        ge = sb("ge", [P, FC, BW])
        gi = sb("gi", [P, 2, 2, BW])
        wqkv = [sb(f"wqkv{i}", [P, CC, 3 * C]) for i in range(LAYERS)]
        wproj = [sb(f"wproj{i}", [P, CC, C]) for i in range(LAYERS)]
        wfc1 = sb("wfc1", [P, CC, MLP])
        wfc2 = sb("wfc2", [P, FC, C])
        col = sb("col", [P, NCOLS])
        row = sb("row", [P, len(ROWV), C])
        gate = sb("gate", [P, B, 4, C])
        gbias = sb("gbias", [P, B, 2, C])
        modc = sb("modc", [P, 12, B])
        l1c = sb("l1c", [P, 4, B])
        cs = sb("cs", [P, CC, B])
        sig = sb("sig", [P, 2, CC, B])
        sc = sb("sc", [P, CC, B])
        vq = sb("vq", [P, B, N], BF16)
        idf = sb("idf", [P, P])
        idb = sb("idb", [P, P], BF16)
        wada = prob[:, :, :, :].rearrange("p a h q -> p (a h q)")[:, 0:CC * 6 * C].rearrange("p (k n) -> p k n", k=CC)
        gef = ge[:, :, :].rearrange("p f t -> p (f t)")
        wg = gef[:, 0:512].rearrange("p (k n) -> p k n", k=CC)
        wb = gef[:, 512:1024].rearrange("p (k n) -> p k n", k=CC)
        scB = gef[:, 1024:1536].rearrange("p (k b n) -> p k b n", k=CC, b=B)
        cB = gef[:, 1536:2048].rearrange("p (k b n) -> p k b n", k=CC, b=B)

        m8 = oraw[:, :, :].rearrange("p t c -> p (t c)").bitcast(U8)[:, 0:B * N].rearrange("p (b n) -> p b n", b=B)
        mk8 = oraw[:, :, :].rearrange("p t c -> p (t c)").bitcast(U8)[0:B, B * N:(B + 1) * N]
        mk = otok[:, :, :].rearrange("p t c -> p (t c)").bitcast(BF16)[0:3, 0:2 * N].rearrange("p (s n) -> p s n", s=2)

        acc = bank("acc")
        banks = [bank(f"bank{i}") for i in range(BANKS)]

        s_x = [[sem(f"s_x{b}{th}") for th in range(2)] for b in range(B)]
        s_cond = sem("s_cond")
        s_small = sem("s_small")
        s_row = sem("s_row")
        s_ada = [sem(f"s_ada{i}") for i in range(2)]
        s_w = {n: sem(f"s_w_{n}") for n in ("qkv0", "qkv1", "proj0", "proj1", "fc1", "fc2")}
        s_id = sem("s_id")
        s_const = sem("s_const")
        s_ones = [sem(f"s_ones{i}") for i in range(SLOTS)]
        s_act0 = sem("s_act0")
        s_dve0 = sem("s_dve0")
        s_mk = sem("s_mk")
        s_mask = sem("s_mask")
        s_acc = sem("s_acc")
        s_mrows = sem("s_mrows")
        s_modc = sem("s_modc")
        s_rows = sem("s_rows")
        job_full = sem("job_full")
        job_act = sem("job_act")
        job_dve = sem("job_dve")
        job_out = {"act": job_act, "dve": job_dve}
        dve_self = sem("dve_self")
        pool_self = sem("pool_self")
        stats_done = sem("stats_done")
        rstd_done = sem("rstd_done")
        xn_done = sem("xn_done")
        biased = sem("biased")
        parts_done = [sem(f"parts_done{i}") for i in range(2)]
        stored = [sem(f"stored{i}") for i in range(2)]
        loaded = [sem(f"loaded{i}") for i in range(SLOTS)]
        st_full = sem("st_full")
        exp_done = sem("exp_done")
        pv_done = sem("pv_done")
        acc_out = sem("acc_out")
        mx_full = sem("mx_full")
        mx_out = sem("mx_out")
        neg_done = sem("neg_done")
        mpart_done = sem("mpart_done")
        mrow_in = [sem(f"mrow_in{i}") for i in range(2)]
        cube_done = sem("cube_done")
        tanh_done = sem("tanh_done")
        gelu_done = sem("gelu_done")
        fin_x = sem("fin_x")
        x_beta = sem("x_beta")
        s_out = [sem(f"s_out{k}") for k in range(4)]

        block = ctx.enter_context(nc.Block())

        def slot(u, g):
            return (u * GROUPS + g) % SLOTS

        def kind(u):
            return u if u < B else 2

        def new_mask(u, g):
            n = u * GROUPS + g
            return n < SLOTS or kind((n - SLOTS) // GROUPS) != kind(u)

        def loads(u, g):
            n = u * GROUPS + g
            before = loads(*divmod(n - SLOTS, GROUPS)) if n >= SLOTS else 0
            return before + 2 * len(BLOCKS) + (2 if new_mask(u, g) else 0)

        def item(u, i):
            return u * ITEMS + i

        def bank_of(e):
            return banks[turn[e] % BANKS]

        def wait_bank(eng, e):
            if turn[e] >= BANKS:
                before = fills[turn[e] - BANKS]
                if before[0] == "st":
                    eng.wait_ge(exp_done, counts[before])
                elif before[0] == "smax":
                    eng.wait_ge(mx_out, counts[before])
                else:
                    job_taken(eng, before)
            return bank_of(e)

        def job_ready(eng, e):
            eng.wait_ge(job_full, jobs[e][0] + 1)
            return bank_of(e)

        def job_taken(eng, e):
            _, w, c = jobs[e]
            eng.wait_ge(job_out[w], c)

        @block.sync
        def _(sp):
            def load_x(b, th):
                sp.dma_start(xs[:, b * TT + 4 * th:b * TT + 4 * th + 4, :],
                             x[b, th * 512:(th + 1) * 512].rearrange("(t p) c -> p t c", p=P)).then_inc(s_x[b][th], 16)

            load_x(0, 0)
            load_x(0, 1)
            ada = adaT.rearrange("(k p) n -> p k n", p=P)
            sp.dma_start(wada[:, :, 0:2 * C], ada[:, :, 0:2 * C]).then_inc(s_ada[0], 16)
            sp.dma_start(wqkv[0][:, :, :], qkvT0.rearrange("(k p) n -> p k n", p=P)).then_inc(s_w["qkv0"], 16)
            sp.dma_start(wada[:, :, 2 * C:6 * C], ada[:, :, 2 * C:6 * C]).then_inc(s_ada[1], 16)
            sp.dma_start(wg, WgT.rearrange("(k p) n -> p k n", p=P)).then_inc(s_ada[1], 16)
            sp.dma_start(wb, WbT.rearrange("(k p) n -> p k n", p=P)).then_inc(s_ada[1], 16)
            load_x(1, 0)
            load_x(1, 1)

            def load_weights():
                for name, dst, src in (("proj0", wproj[0], projT0), ("fc1", wfc1, fc1T), ("fc2", wfc2, fc2T),
                                       ("qkv1", wqkv[1], qkvT1), ("proj1", wproj[1], projT1)):
                    sp.dma_start(dst[:, :, :], src.rearrange("(k p) n -> p k n", p=P)).then_inc(s_w[name], 16)

            def store_parts(u, j):
                n = counts[("qk", u, j)]
                sp.wait_ge(parts_done[(n - 1) % 2], (n + 1) // 2)
                if u >= 2 and j == 0:
                    for g in range(GROUPS):
                        sp.wait_ge(loaded[slot(u - 2, g)], 16 * loads(u - 2, g))
                side, cc, th = j // 4, j // 2 % 2, j % 2
                dst = scratch[u % 2, side, :, cc * P:(cc + 1) * P, th * 512:(th + 1) * 512]
                sp.dma_start(dst.rearrange("r c n -> c r n"), parts[:, (n - 1) % 2, :, :]).then_inc(stored[(n - 1) % 2], 16)

            def load_group(u, g):
                s = slot(u, g)
                jn = counts[("qk", u, 5 if g < 2 else 7)]
                for k in range(2):
                    sp.wait_ge(stored[k], 16 * (jn // 2))
                n = u * GROUPS + g
                if n == 0:
                    sp.wait_ge(s_mrows, 16)
                if n < SLOTS:
                    sp.wait_ge(s_ones[n], 1)
                if n >= SLOTS:
                    pu, pg = divmod(n - SLOTS, GROUPS)
                    sp.wait_ge(st_full, counts[("st", pu, 2 * pg + 1, 7, 3)])
                    sp.wait_ge(mx_full, counts[("smax", pu, 2 * pg + 1, 31)])
                group = slice(g * HG * HD, (g + 1) * HG * HD)
                r0 = 0
                for r, w in enumerate(BLOCKS):
                    q = scratch[u % 2, 0, r:r + 1, group, :].rearrange("r (d h) n -> d r (h n)", d=HD)
                    k = scratch[u % 2, 1, 0:w, group, :].rearrange("r (d h) n -> d r (h n)", d=HD)
                    for dst, src in ((qs[s], q.to_broadcast([HD, w, HG * N])), (ks[s], k)):
                        sp.dma_start(dst[r0:r0 + w * HD, :, :].rearrange("p h n -> p (h n)"), src).then_inc(loaded[s], 16)
                    r0 += w * HD
                if new_mask(u, g):
                    m = kind(u)
                    for side, dst in enumerate((qs[s], ks[s])):
                        sp.dma_start(dst[ROW_MASK:ROW_MASK + 1, :, :],
                                     mask_rows[m:m + 1, side:side + 1, :].to_broadcast([1, HG, N])).then_inc(loaded[s], 16)

            def put_max(u, i):
                e = ("mrow", u, i)
                job_taken(sp, e)
                s, qh = slot(u, i // 2), i % 2
                k = item(u, i) % 2
                for part in range(3):
                    sp.dma_start(qs[s][ROW_MAX + part:ROW_MAX + part + 1, :, qh * QW:(qh + 1) * QW],
                                 mrow[part * HG:(part + 1) * HG, k, :]).then_inc(mrow_in[k], 16)

            for e in plan:
                if e[0] == "mask":
                    sp.wait_ge(s_mask, 1)
                    sp.dma_start(mask_rows, mk).then_inc(s_mrows, 16)
                elif e[0] == "qk":
                    store_parts(e[1], e[2])
                elif e[0] == "mrow":
                    put_max(e[1], e[2])
                elif e[0] == "fin":
                    _, u, t = e
                    sp.wait_ge(fin_x, counts[e])
                    sp.dma_start(out[u % B, t * P:(t + 1) * P, :], xn[:, t % 4, :]).then_inc(s_out[t % 4], 16)
                elif e[0] == "load":
                    load_group(e[1], e[2])
                elif e[0] == "weights":
                    load_weights()
            for k in range(4):
                sp.wait_ge(s_out[k], 16 * B * TT // 4)

        @block.tensor
        def _(pe):
            def mod(part):
                if part == 0:
                    pe.wait_ge(s_dve0, 1)
                pe.wait_ge(s_ada[part], (16, 48)[part])
                bank_ = wait_bank(pe, ("mod", part))
                chunks = ([(wada, sc, m) for m in (0, 1, 2, 3)],
                          [(wada, sc, m) for m in (6, 7, 8, 9)] + [(wg, cs, 0), (wg, cs, 1), (wb, cs, 0), (wb, cs, 1)])[part]
                for n, (w, v, m) in enumerate(chunks):
                    for k in range(CC):
                        mm = pe.matmul(bank_[:, n * B:(n + 1) * B], w[:, k, m * P:(m + 1) * P], v[:, k, :],
                                       start=(k == 0), stop=(k == CC - 1))
                mm.then_inc(job_full, 1)

            def rows_(b, n):
                bank_ = wait_bank(pe, ("rows", b, n))
                pe.wait_ge(s_dve0, 2)
                w, v = ((wada[:, :, 2 * C:3 * C], scB), (wada[:, :, 5 * C:6 * C], scB), (wg, cB), (wb, cB))[n]
                for k in range(CC):
                    mm = pe.matmul(bank_[:, 0:C], v[:, k, b, :], w[:, k, :], start=(k == 0), stop=(k == CC - 1))
                mm.then_inc(job_full, 1)

            def lnT(e):
                _, u, k, th, cc = e
                bank_ = wait_bank(pe, e)
                pe.wait_ge(xn_done, 4 * counts[("xn", u, k, th)])
                for t in range(4):
                    mm = pe.transpose(bank_[:, t * P:(t + 1) * P], xn[:, t, cc * P:(cc + 1) * P], idf[:, :])
                mm.then_inc(job_full, 1)

            def qk(e):
                _, u, j = e
                side, cc, th = j // 4, j // 2 % 2, j % 2
                bank_ = wait_bank(pe, e)
                pe.wait_ge(s_w[f"qkv{u // B}"], 16)
                job_taken(pe, ("lnT", u, 0, th, CC - 1))
                for k in range(CC):
                    mm = pe.matmul(bank_[:, :], wqkv[u // B][:, k, side * C + cc * P:side * C + (cc + 1) * P],
                                   hT[:, k, th * 512:(th + 1) * 512], start=(k == 0), stop=(k == CC - 1))
                mm.then_inc(job_full, 1)

            def v(e):
                _, u, t = e
                bank_ = wait_bank(pe, e)
                for k in range(CC):
                    mm = pe.matmul(bank_[:, 0:C], hT[:, k, t * P:(t + 1) * P], wqkv[u // B][:, k, 2 * C:3 * C],
                                   start=(k == 0), stop=(k == CC - 1))
                mm.then_inc(job_full, 1)

            def smax(e):
                _, u, i, m = e
                n = counts[e]
                h, qt, kh = m // 8, m // 2 % 4, m % 2
                s, q0 = slot(u, i // 2), (i % 2) * QW + qt * P
                if m == 0:
                    pe.wait_ge(loaded[s], 16 * loads(u, i // 2))
                pe.matmul(wait_bank(pe, e)[:, :], qs[s][0:ROW_MAX, h, q0:q0 + P], ks[s][0:ROW_MAX, h, kh * 512:(kh + 1) * 512],
                          start=True, stop=True).then_inc(mx_full, 1)

            def mrow_(e):
                bank_ = wait_bank(pe, e)
                k = item(e[1], e[2]) % 2
                pe.wait_ge(mpart_done, item(e[1], e[2]) + 1)
                for t in range(TQ):
                    mm = pe.matmul(bank_[0:3 * HG, t * P:(t + 1) * P],
                                   mpart[:, k, :, :].rearrange("p r (h t) -> p (r h) t", t=TQ)[:, :, t], idb[:, :],
                                   start=True, stop=True)
                mm.then_inc(job_full, 1)

            def st(e):
                _, u, i, s, h = e
                n = counts[e]
                sl, q0 = slot(u, i // 2), (i % 2) * QW
                if s == 0 and h == 0:
                    k = item(u, i)
                    pe.wait_ge(mrow_in[k % 2], 48 * (k // 2 + 1))
                pe.matmul(wait_bank(pe, e)[:, :], ks[sl][0:ROWS, h, s * P:(s + 1) * P], qs[sl][0:ROWS, h, q0:q0 + QW],
                          start=True, stop=True).then_inc(st_full, 1)

            def pv(e):
                _, u, i, s = e
                n = counts[e]
                pe.wait_ge(exp_done, HG * n)
                if i == 0:
                    job_taken(pe, ("v", u, s))
                if s == 0:
                    if item(u, i) > 0:
                        pe.wait_ge(acc_out, item(u, i))
                    else:
                        pe.wait_ge(s_acc, 1)
                for h in range(HG):
                    mm = pe.matmul(acc[h * CW:h * CW + VW, :], va[:, s, (i // 2) * HG + h, :], prob[:, (n - 1) % 2, h, :],
                                   start=(s == 0), stop=(s == KT - 1), skip_group_check=True)
                mm.then_inc(pv_done, 1)

            def oT_(e):
                bank_ = wait_bank(pe, e)
                n = item(e[1], e[2])
                pe.wait_ge(acc_out, n + 1)
                for t in range(TQ):
                    mm = pe.transpose(bank_[:, t * P:(t + 1) * P], oraw[:, n % 2, t * P:(t + 1) * P], idf[:, :])
                mm.then_inc(job_full, 1)

            def opT(e):
                _, u, th, cc = e
                bank_ = wait_bank(pe, e)
                job_taken(pe, ("oT", u, ITEMS - 2 + th))
                for t in range(4):
                    mm = pe.transpose(bank_[:, t * P:(t + 1) * P], otok[:, 4 * th + t, cc * P:(cc + 1) * P], idf[:, :])
                mm.then_inc(job_full, 1)

            def proj(e):
                _, u, t = e
                bank_ = wait_bank(pe, e)
                pe.wait_ge(s_w[f"proj{u // B}"], 16)
                job_taken(pe, ("opT", u, t // 4, CC - 1))
                for k in range(CC):
                    mm = pe.matmul(bank_[:, 0:C], oT[:, k, t * P:(t + 1) * P], wproj[u // B][:, k, :],
                                   start=(k == 0), stop=(k == CC - 1))
                mm.then_inc(job_full, 1)

            def fc1(e):
                _, u, tb, f2 = e
                bank_ = wait_bank(pe, e)
                pe.wait_ge(s_w["fc1"], 16)
                job_taken(pe, ("lnT", u, 1, tb // 2, CC - 1))
                for f in range(2):
                    for k in range(CC):
                        c0 = (2 * f2 + f) * P
                        mm = pe.matmul(bank_[:, f * BW:(f + 1) * BW], wfc1[:, k, c0:c0 + P], hT[:, k, tb * BW:(tb + 1) * BW],
                                       start=(k == 0), stop=(k == CC - 1))
                mm.then_inc(job_full, 1)

            def fc2(e):
                _, u, tb, t = e
                bank_ = wait_bank(pe, e)
                pe.wait_ge(s_w["fc2"], 16)
                pe.wait_ge(gelu_done, counts[("gelu", u, tb, FC // 2 - 1)])
                for f in range(FC):
                    mm = pe.matmul(bank_[:, 0:C], ge[:, f, t * P:(t + 1) * P], wfc2[:, f, :], start=(f == 0), stop=(f == FC - 1))
                mm.then_inc(job_full, 1)

            pe.wait_ge(s_id, 2)
            does = dict(lnT=lnT, qk=qk, v=v, smax=smax, mrow=mrow_, st=st, pv=pv, oT=oT_, opT=opT, proj=proj, fc1=fc1, fc2=fc2)
            for e in plan:
                if e[0] == "mod":
                    mod(e[1])
                elif e[0] == "rows":
                    rows_(e[1], e[2])
                elif e[0] in does:
                    does[e[0]](e)

        @block.scalar
        def _(act):
            act.dma_start(cs[:, :, :], cT.rearrange("(k p) b -> p k b", p=P)).then_inc(s_cond, 16)
            act.dma_start(col[:, :], cols).then_inc(s_cond, 16)
            act.dma_start(mk8, mask).then_inc(s_small, 16)
            act.dma_start(m8, mask.rearrange("(o b) n -> o b n", o=1).to_broadcast([P, B, N])).then_inc(s_small, 16)
            act.wait_ge(s_cond, 32)
            act.activation(sig[:, 0, :, :], cs[:, :, :], ACT.Exp, scale=-1.0).then_inc(s_act0, 1)
            act.dma_start(row[:, :, :], rows.rearrange("(o r) c -> o r c", o=1).to_broadcast([P, len(ROWV), C])).then_inc(s_row, 16)

            def lnT(e):
                _, u, k, th, cc = e
                if u == 0:
                    act.wait_ge(s_modc, k + 1)
                if u < B:
                    a, b_ = modc[:, 4 * k + 2 + cc, u % B:u % B + 1], modc[:, 4 * k + cc, u % B:u % B + 1]
                else:
                    a, b_ = l1c[:, cc, u % B:u % B + 1], l1c[:, 2 + cc, u % B:u % B + 1]
                bank_ = job_ready(act, e)
                act.activation(hT[:, cc, th * 512:(th + 1) * 512], bank_[:, :], ACT.Identity, bias=b_, scale=a).then_inc(job_act, 1)

            def qk(e):
                _, u, j = e
                n = counts[e]
                side, cc = j // 4, j // 2 % 2
                c0 = COLS[f"qk{u // B}"] + 2 * side + cc
                bank_ = job_ready(act, e)
                if n > 2:
                    act.wait_ge(parts_done[(n - 1) % 2], (n - 1) // 2)
                act.activation(qf[:, (n - 1) % 2, :], bank_[:, :], ACT.Identity, bias=col[:, c0:c0 + 1]).then_inc(job_act, 1)

            def mrow_(e):
                k = item(e[1], e[2])
                bank_ = job_ready(act, e)
                if k >= 2:
                    act.wait_ge(mrow_in[k % 2], 48 * (k // 2))
                act.activation(mrow[:, k % 2, :], bank_[0:3 * HG, :], ACT.Identity).then_inc(job_act, 1)

            def st(e):
                _, u, i, s, h = e
                n = counts[e]
                step = (n - 1) // HG
                act.wait_ge(st_full, n)
                if step >= 2:
                    act.wait_ge(pv_done, step - 1)
                act.activation(prob[:, step % 2, h, :], bank_of(e)[:, :], ACT.Exp).then_inc(exp_done, 1)

            def evac(e):
                n = item(e[1], e[2])
                act.wait_ge(pv_done, KT * (n + 1))
                if n >= 2:
                    job_taken(act, ("oT", *divmod(n - 2, ITEMS)))
                act.activation(oraw[:, n % 2, :], acc[:, :], ACT.Identity).then_inc(acc_out, 1)

            def opT(e):
                _, u, th, cc = e
                bank_ = job_ready(act, e)
                act.activation(oT[:, cc, th * 512:(th + 1) * 512], bank_[:, :], ACT.Identity).then_inc(job_act, 1)

            def fc1(e):
                _, u, tb, f2 = e
                bank_ = job_ready(act, e)
                if u == 0 and tb == 0 and f2 == 0:
                    act.wait_ge(s_rows, 1)
                if tb > 0:
                    act.wait_ge(job_full, jobs[("fc2", u, tb - 1, 1)][0] + 1)
                n = counts[e]
                if n > 2:
                    act.wait_ge(gelu_done, n - 2)
                for k in range(2):
                    b_ = col[:, COLS["fc1"] + 2 * f2 + k:COLS["fc1"] + 2 * f2 + k + 1]
                    act.activation(gi[:, (n - 1) % 2, k, :], bank_[:, k * BW:(k + 1) * BW], ACT.Square, bias=b_)
                    i = act.activation(ge[:, 2 * f2 + k, :], bank_[:, k * BW:(k + 1) * BW], ACT.Identity, bias=b_)
                i.then_inc(job_act, 1)

            def tanh(e):
                n = counts[e]
                g = gi[:, (n - 1) % 2, :, :]
                act.wait_ge(cube_done, n)
                act.activation(g, g, ACT.Tanh, scale=GELU_SCALE).then_inc(tanh_done, 1)

            does = dict(lnT=lnT, mrow=mrow_, st=st, evac=evac, opT=opT, fc1=fc1, tanh=tanh)
            for e in plan:
                if e[0] in does:
                    does[e[0]](e)
                elif e[0] == "qk" and taker(e) == "act":
                    qk(e)

        @block.vector
        def _(dve):
            own = [0]

            def link(ins):
                own[0] += 1
                ins.then_inc(dve_self, 1)
                dve.wait_ge(dve_self, own[0])

            R = {n: row[:, k, :] for k, n in enumerate(ROWV)}

            def silu():
                dve.wait_ge(s_act0, 1)
                link(dve.tensor_scalar(sig[:, 1, :, :], sig[:, 0, :, :], 1.0, None, ALU.add))
                link(dve.reciprocal(sig[:, 0, :, :], sig[:, 1, :, :]))
                dve.tensor_tensor(sc[:, :, :], cs[:, :, :], sig[:, 0, :, :], ALU.mult).then_inc(s_dve0, 1)

            def quarter():
                dve.wait_ge(s_small, 32)
                link(dve.tensor_scalar(vq[:, :, :], m8, float(HD) ** -0.5, None, ALU.mult))

            def mask_():
                dve.wait_ge(s_mk, 2)
                dve.tensor_copy(mk[0:B, 0, :], mk8)
                dve.tensor_scalar(mk[0:B, 1, :], mk8, -1.0, -MASKED, ALU.add, ALU.mult).then_inc(s_mask, 1)
                dve.tensor_copy(scB, sc[:, :, :].rearrange("p k (b o) -> p k b o", o=1).to_broadcast([P, CC, B, P]))
                dve.tensor_copy(cB, cs[:, :, :].rearrange("p k (b o) -> p k b o", o=1).to_broadcast([P, CC, B, P])).then_inc(s_dve0, 1)
                dve.memset(acc[:, :], 0.0).then_inc(s_acc, 1)

            def mod(part):
                bank_ = job_ready(dve, ("mod", part))
                m = slice(4 * part, 4 + 8 * part)
                w = m.stop - m.start
                bias = col[:, COLS["mod"] + m.start:COLS["mod"] + m.stop].rearrange("p (n o) -> p n o", o=1).to_broadcast([P, w, B])
                dve.tensor_tensor(modc[:, m, :], bank_[:, 0:w * B].rearrange("p (n b) -> p n b", b=B), bias, ALU.add).then_inc(job_dve, 1)
                dve.wait_ge(job_dve, jobs[("mod", part)][2])
                i = dve.tensor_scalar(modc[:, 4 * part + 2:4 * part + 4, :], modc[:, 4 * part + 2:4 * part + 4, :], 1.0, None, ALU.add)
                if part == 0:
                    i.then_inc(s_modc, 1)
                else:
                    for cc in range(CC):
                        g, b_ = (col[:, COLS[n] + cc:COLS[n] + cc + 1] for n in ("lng", "lnb"))
                        dve.tensor_scalar(l1c[:, cc, :], modc[:, 8 + cc, :], g, None, ALU.mult)
                        link(dve.tensor_scalar(l1c[:, 2 + cc, :], modc[:, 8 + cc, :], b_, None, ALU.mult))
                    dve.tensor_tensor(l1c[:, 2:4, :], l1c[:, 2:4, :], modc[:, 10:12, :], ALU.add).then_inc(s_modc, 1)

            def rows_(b, n):
                e = ("rows", b, n)
                bank_ = job_ready(dve, e)
                dve.wait_ge(s_row, 16)
                name = ("gate_msa", "gate_mlp", "gamma", "beta")[n]
                dve.tensor_tensor(gate[:, b, n, :], bank_[:, 0:C], R[name], ALU.add).then_inc(job_dve, 1)
                dve.wait_ge(job_dve, jobs[e][2])
                if n < 2:
                    link(dve.tensor_tensor(gbias[:, b, n, :], gate[:, b, n, :], R[("proj0", "fc2")[n]], ALU.mult))
                if n == 1:
                    link(dve.tensor_scalar(gate[:, b, n, :], gate[:, b, n, :], 0.5, None, ALU.mult))
                if n == 3:
                    link(dve.tensor_tensor(tmp[:, 0, :], gate[:, b, 2, :], R["ln_b"], ALU.mult))
                    link(dve.tensor_tensor(gate[:, b, 3, :], gate[:, b, 3, :], tmp[:, 0, :], ALU.add))
                    i = dve.tensor_tensor(gate[:, b, 2, :], gate[:, b, 2, :], R["ln_g"], ALU.mult)
                    link(i)
                    if b == B - 1:
                        dve.memset(rec[:, :, :, :], 0.0).then_inc(s_rows, 1)

            def stats(e):
                _, u, k, th = e
                b = u % B
                if k == 1 and u >= B:
                    return
                if k == 0 and u < B:
                    dve.wait_ge(s_x[b][th], 16)
                for t in range(4 * th, 4 * th + 4):
                    i = dve.bn_stats(stat[:, t, :], xs[:, b * TT + t, :])
                link(i)
                for t in range(4 * th, 4 * th + 4):
                    i = dve.bn_aggr(mv[:, t, :], stat[:, t, :])
                i.then_inc(stats_done, 1)
                dve.wait_ge(stats_done, counts[e])

            def xn_(e):
                _, u, k, th = e
                dve.wait_ge(rstd_done, counts[("stats", u, k, th)])
                n = counts[e]
                if n > 1:
                    prev = [p for p in plan[:plan.index(e)] if p[0] == "lnT"][-1]
                    dve.wait_ge(job_full, jobs[prev][0] + 1)
                if th == 0 and (before := sum(p[0] == "fin" for p in plan[:plan.index(e)])):
                    for k4 in range(4):
                        dve.wait_ge(s_out[k4], 16 * before // 4)
                for t in range(4):
                    tt = 4 * th + t
                    dve.tensor_scalar(xn[:, t, :], xs[:, (u % B) * TT + tt, :], mv[:, tt, 0:1], rstd[:, 1, tt:tt + 1],
                                      ALU.subtract, ALU.mult).then_inc(xn_done, 1)

            def qk(e):
                _, u, j = e
                n = counts[e]
                cc, th = j // 2 % 2, j % 2
                c0 = COLS["qk0"] + cc
                bank_ = job_ready(dve, e)
                if n > 2:
                    dve.wait_ge(parts_done[(n - 1) % 2], (n - 1) // 2)
                dve.scalar_tensor_tensor(out=qf[:, (n - 1) % 2, :], in0=bank_[:, :], scalar=col[:, c0:c0 + 1],
                                         in1=vq[:, u, th * 512:(th + 1) * 512], op0=ALU.add, op1=ALU.mult).then_inc(job_dve, 1)

            def split(e):
                n = counts[e]
                k = (n - 1) % 2
                job_taken(dve, e)
                if n > 2:
                    dve.wait_ge(stored[k], 16 * ((n - 1) // 2))
                f = qf[:, k, :]
                link(dve.tensor_scalar(parts[:, k, 0, :], f, 1.0, 0.0, ALU.mult, ALU.add))
                link(dve.tensor_tensor(f, f, parts[:, k, 0, :], ALU.subtract))
                link(dve.tensor_scalar(parts[:, k, 1, :], f, 1.0, 0.0, ALU.mult, ALU.add))
                dve.tensor_tensor(parts[:, k, 2, :], f, parts[:, k, 1, :], ALU.subtract).then_inc(parts_done[k], 1)

            def v(e):
                _, u, t = e
                bank_ = job_ready(dve, e)
                if u == 0 and t == 0:
                    dve.wait_ge(s_row, 16)
                if u > 0:
                    dve.wait_ge(pv_done, counts[("pv", u - 1, ITEMS - 1, t)])
                dve.tensor_tensor(va[:, t, :, 0:HD], bank_[:, 0:C].rearrange("p (h d) -> p h d", h=H),
                                  R[f"v{u // B}"].rearrange("p (h d) -> p h d", h=H), ALU.add).then_inc(job_dve, 1)

            def smax(e):
                _, u, i, m = e
                n = counts[e]
                dve.wait_ge(mx_full, n)
                dve.tensor_reduce(mx[:, item(u, i) % 2, m // 2, m % 2:m % 2 + 1], bank_of(e)[:, :], AX.X, ALU.max).then_inc(mx_out, 1)

            def neg(e):
                k = item(e[1], e[2])
                dve.wait_ge(mx_out, counts[("smax", e[1], e[2], 31)])
                if k >= 2:
                    dve.wait_ge(mpart_done, k - 1)
                dve.tensor_reduce(negm[:, k % 2, :], mx[:, k % 2, :, :], AX.X, ALU.max, negate=True).then_inc(neg_done, 1)
                dve.wait_ge(neg_done, k + 1)

            def oT_(e):
                _, u, i = e
                k = item(u, i)
                bank_ = job_ready(dve, e)
                o = bank_[:, :].rearrange("p (t h w) -> p t h w", t=TQ, w=CW)
                r = rec[:, k % 2, :, :]
                link(dve.reciprocal(r, o[:, :, :, HD]))
                if u >= B:
                    link(dve.tensor_scalar(r, r, float(C) ** -0.5, None, ALU.mult))
                g, qh = i // 2, i % 2
                if i < 2 and u > 0:
                    dve.wait_ge(job_full, jobs[("opT", u - 1, i, CC - 1)][0] + 1)
                dst = otok[:, qh * TQ:(qh + 1) * TQ, g * HG * HD:(g + 1) * HG * HD].rearrange("p t (h d) -> p t h d", h=HG)
                dve.tensor_tensor(dst, o[:, :, :, 0:HD], r.rearrange("p t (h o) -> p t h o", o=1).to_broadcast([P, TQ, HG, HD]),
                                  ALU.mult).then_inc(job_dve, 1)

            def residual(e, t, k):
                u = e[1]
                bank_ = job_ready(dve, e)
                xt = xs[:, (u % B) * TT + t, :]
                if t % 4 == 0:
                    dve.wait_ge(biased, counts[("bias_in", u, k, t // 4)])
                if u < B:
                    link(dve.tensor_tensor(tmp[:, t % 2, :], bank_[:, 0:C], gate[:, u % B, k, :], ALU.mult))
                    dve.tensor_tensor(xt, tmp[:, t % 2, :], xt, ALU.add).then_inc(job_dve, 1)
                else:
                    dve.tensor_tensor(xt, bank_[:, 0:C], xt, ALU.add).then_inc(job_dve, 1)
                    dve.wait_ge(job_dve, jobs[e][2])
                    link(dve.bn_stats(stat[:, t, :], xt))
                    i = dve.bn_aggr(mv[:, t, :], stat[:, t, :])
                    if t % 4 == 3:
                        n = counts[("stats", u, 1, t // 4)]
                        i.then_inc(stats_done, 1)
                        dve.wait_ge(stats_done, n)
                if t % 4 == 3:
                    dve.wait_ge(job_dve, jobs[e][2])

            def gelu(e):
                _, u, tb, f2 = e
                n = counts[e]
                dve.wait_ge(tanh_done, n)
                y = ge[:, 2 * f2:2 * f2 + 2, :]
                dve.scalar_tensor_tensor(out=y, in0=gi[:, (n - 1) % 2, :, :], scalar=1.0, in1=y, op0=ALU.add,
                                         op1=ALU.mult).then_inc(gelu_done, 1)

            def fin(e):
                _, u, t = e
                b = u % B
                k = t % 4
                n = counts[e]
                if n > 4:
                    dve.wait_ge(s_out[k], 16 * ((n - 1) // 4))
                    dve.wait_ge(fin_x, n - 4)
                link(dve.scalar_tensor_tensor(out=xn[:, k, :], in0=xs[:, b * TT + t, :], scalar=mv[:, t, 0:1], in1=gate[:, b, 2, :],
                                              op0=ALU.subtract, op1=ALU.mult))
                if t % 4 == 0:
                    dve.wait_ge(rstd_done, counts[("stats", u, 1, t // 4)])
                dve.wait_ge(x_beta, (u - B) * TT + t + 1)
                dve.scalar_tensor_tensor(out=xn[:, k, :], in0=xn[:, k, :], scalar=rstd[:, 1, t:t + 1], in1=ge[:, t, :],
                                         op0=ALU.mult, op1=ALU.add).then_inc(fin_x, 1)

            first = dict(silu=silu, quarter=quarter, mask=mask_)
            does = dict(stats=stats, xn=xn_, v=v, smax=smax, neg=neg, oT=oT_, fin=fin, gelu=gelu)
            for e in plan:
                if e[0] == "mod":
                    mod(e[1])
                elif e[0] == "rows":
                    rows_(e[1], e[2])
                elif e[0] == "proj":
                    residual(e, e[2], 0)
                elif e[0] == "fc2":
                    residual(e, 2 * e[2] + e[3], 1)
                elif e[0] == "qk":
                    if taker(e) == "dve":
                        qk(e)
                    if splitter(e) == "dve":
                        split(e)
                elif e[0] in does:
                    does[e[0]](e)
                elif e[0] in first:
                    first[e[0]]()

        @block.gpsimd
        def _(pool):
            own = [0]

            def link(ins):
                own[0] += 1
                ins.then_inc(pool_self, 1)
                pool.wait_ge(pool_self, own[0])

            link(pool.memset(idf[:, :], 0.0))
            pool.affine_select(out=idf[:, :], in_=idf[:, :], compare_op=ALU.not_equal, fill=1.0, base=0,
                               pattern=[[-1, P]], channel_multiplier=1).then_inc(s_id, 1)
            pool.wait_ge(s_id, 1)
            pool.tensor_copy(idb[:, :], idf[:, :]).then_inc(s_id, 1)
            pool.wait_ge(s_id, 2)
            pool.memset(power[:, :], -0.5).then_inc(s_const, 1)
            pool.wait_ge(s_const, 1)
            pool.memset(mk[:, 0, :], 1.0).then_inc(s_mk, 1)
            pool.wait_ge(s_mk, 1)
            pool.memset(mk[:, 1, :], 0.0).then_inc(s_mk, 1)
            pool.wait_ge(s_mk, 2)
            pool.memset(ks[0][ROW_MASK:ROWS, :, :], 1.0).then_inc(s_ones[0], 1)
            pool.wait_ge(s_ones[0], 1)

            def ones(s):
                pool.wait_ge(rstd_done, counts[("stats", 0, 0, 1)])
                if s == 2:
                    n = counts[("qk", 0, 1)]
                    pool.wait_ge(parts_done[(n - 1) % 2], (n + 1) // 2)
                pool.memset(ks[s][ROW_MASK:ROWS, :, :], 1.0).then_inc(s_ones[s], 1)
                pool.wait_ge(s_ones[s], 1)

            link(pool.memset(va[:, :, :, HD:VW], 1.0))

            def stats(e):
                _, u, k, th = e
                ts = slice(4 * th, 4 * th + 4)
                pool.wait_ge(stats_done, counts[e])
                pool.wait_ge(s_const, 1)
                readers = [p for p in plan[:plan.index(e)] if p[0] == "fin" and p[2] // 4 == th or p[0] == "xn" and p[3] == th]
                if readers and readers[-1][0] == "xn":
                    pool.wait_ge(xn_done, 4 * counts[readers[-1]])
                elif readers:
                    pool.wait_ge(fin_x, counts[readers[-1]])
                link(pool.tensor_scalar(rstd[:, 0, ts], mv[:, ts, 1], EPS[u // B], 1.0, ALU.add, ALU.mult))
                pool.tensor_tensor(rstd[:, 1, ts], rstd[:, 0, ts], power[:, ts], ALU.pow).then_inc(rstd_done, 1)

            def proj(e):
                _, u, t = e
                job_taken(pool, e)
                if u > B:
                    pool.wait_ge(fin_x, counts[("fin", u - 1, t)])
                pool.tensor_tensor(ge[:, t, :], xs[:, (u % B) * TT + t, :], gate[:, u % B, 3, :], ALU.add).then_inc(x_beta, 1)

            def split(e):
                n = counts[e]
                k = (n - 1) % 2
                job_taken(pool, e)
                if n > 2:
                    pool.wait_ge(stored[k], 16 * ((n - 1) // 2))
                f = qf[:, k, :]
                link(pool.tensor_scalar(parts[:, k, 0, :], f, 1.0, 0.0, ALU.mult, ALU.add))
                link(pool.tensor_tensor(f, f, parts[:, k, 0, :], ALU.subtract))
                link(pool.tensor_scalar(parts[:, k, 1, :], f, 1.0, 0.0, ALU.mult, ALU.add))
                pool.tensor_tensor(parts[:, k, 2, :], f, parts[:, k, 1, :], ALU.subtract).then_inc(parts_done[k], 1)

            def neg(e):
                n = item(e[1], e[2])
                k = n % 2
                pool.wait_ge(neg_done, n + 1)
                if n >= 2:
                    pool.wait_ge(job_full, jobs[("mrow", *divmod(n - 2, ITEMS))][0] + 1)
                f = negm[:, k, :]
                link(pool.tensor_scalar(mpart[:, k, 0, :], f, 1.0, 0.0, ALU.mult, ALU.add))
                link(pool.tensor_tensor(f, f, mpart[:, k, 0, :], ALU.subtract))
                link(pool.tensor_scalar(mpart[:, k, 1, :], f, 1.0, 0.0, ALU.mult, ALU.add))
                pool.tensor_tensor(mpart[:, k, 2, :], f, mpart[:, k, 1, :], ALU.subtract).then_inc(mpart_done, 1)

            def bias_in(e):
                _, u, k, th = e
                pool.wait_ge(xn_done, 4 * counts[("xn", u, k, th)])
                if u == 0 and k == 0:
                    pool.wait_ge(s_rows, 1)
                bias = gbias[:, u % B, k, :] if u < B else row[:, ROWV.index("proj1"), :]
                for t in range(4 * th, 4 * th + 4):
                    xt = xs[:, (u % B) * TT + t, :]
                    i = pool.tensor_tensor(xt, xt, bias, ALU.add)
                i.then_inc(biased, 1)

            def fc1(e):
                _, u, tb, f2 = e
                n = counts[e]
                g = gi[:, (n - 1) % 2, :, :]
                job_taken(pool, e)
                link(pool.tensor_scalar(g, g, GELU_CUBE, 1.0, ALU.mult, ALU.add))
                pool.tensor_tensor(g, g, ge[:, 2 * f2:2 * f2 + 2, :], ALU.mult).then_inc(cube_done, 1)

            does = dict(stats=stats, neg=neg, bias_in=bias_in, fc1=fc1)
            for e in plan:
                if e[0] in does:
                    does[e[0]](e)
                elif e[0] == "qk" and splitter(e) == "pool":
                    split(e)
                elif e[0] in ("quarter", "mask"):
                    ones(1 if e[0] == "quarter" else 2)
                elif e[0] == "proj" and e[1] >= B:
                    proj(e)


def kernel(**inputs):
    import numpy as np
    import concourse.bacc as bacc
    from concourse.bass_utils import run_bass_kernel_spmd

    a = {n: np.asarray(v) for n, v in inputs.items()}

    def t(w):
        return np.ascontiguousarray(w.T)

    def chunks(v):
        return v.reshape(-1, P).T

    def by_group(w):
        return w.reshape(-1, GROUPS, HG, HD).transpose(0, 1, 3, 2).reshape(-1, C)

    def grouped(w):
        return np.concatenate([by_group(w[:, :C]), by_group(w[:, C:2 * C]), w[:, 2 * C:]], axis=1)

    w1 = a["L1_cond_Wqkv"].reshape(C, 3, C).transpose(1, 0, 2).reshape(3 * C, C)
    b1 = a["L1_cond_bqkv"].reshape(C, 3).T.reshape(3 * C)
    b0, ada = a["L0_cond_qkv_b"], a["L0_cond_ada_b"].reshape(6, C)
    cols = np.concatenate([
        chunks(grouped(b0[None])[0, :2 * C]), chunks(grouped(b1[None])[0, :2 * C]), chunks(a["L0_cond_fc1_b"]),
        chunks(ada[0]), chunks(ada[1]), chunks(ada[3]), chunks(ada[4]), chunks(a["L1_cond_bg"]), chunks(a["L1_cond_bb"]),
        chunks(a["L1_cond_ln_g"]), chunks(a["L1_cond_ln_b"])], axis=1)
    rows = np.stack([b0[2 * C:], b1[2 * C:], a["L0_cond_proj_b"], a["L1_cond_bp"], a["L0_cond_fc2_b"], ada[2], ada[5],
                     a["L1_cond_bg"], a["L1_cond_bb"], a["L1_cond_ln_g"], a["L1_cond_ln_b"]])
    arrays = {
        "x": a["x"], "cT": t(a["cond_1024"]), "mask": a["mask_BxS_bk1"],
        "adaT": t(a["L0_cond_ada_w"]), "WgT": t(a["L1_cond_Wg"]), "WbT": t(a["L1_cond_Wb"]),
        "qkvT0": grouped(t(a["L0_cond_qkv_w"])), "qkvT1": grouped(t(w1)), "projT0": t(a["L0_cond_proj_w"]), "projT1": t(a["L1_cond_Wp"]),
        "fc1T": t(a["L0_cond_fc1_w"]), "fc2T": t(a["L0_cond_fc2_w"]), "cols": cols, "rows": rows,
    }
    arrays = {f"in_{n}": np.ascontiguousarray(v) for n, v in arrays.items()}
    nc = bacc.Bacc("TRN2", target_bir_lowering=False, num_devices=1)
    args = [nc.dram_tensor(n, v.shape, mybir.dt.from_np(v.dtype), kind="ExternalInput").ap() for n, v in arrays.items()]
    args.append(nc.dram_tensor("out_0", (B, N, C), F32, kind="ExternalOutput").ap())
    build(nc, *args)
    r = run_bass_kernel_spmd(nc, [arrays], core_ids=[0])
    return r.results[0]["out_0"]
```

```python
import math
from contextlib import ExitStack

import concourse.bass as bass
from concourse import mybir

ALU = mybir.AluOpType
ACT = mybir.ActivationFunctionType
AX = mybir.AxisListType
F32 = mybir.dt.float32
BF16 = mybir.dt.bfloat16
U8 = mybir.dt.uint8

P = 128
B, N, C = 2, 1024, 256
H, HD = 16, 16
MLP = 4 * C
TT = N // P
CC = C // P
HG = 4
GROUPS = H // HG
QW = 512
QH = N // QW
TQ = QW // P
KT = N // P
ITEMS = GROUPS * QH
STEPS = ITEMS * KT
FC = MLP // P
TB = 4
BW = N // TB
LAYERS = 2
UNITS = LAYERS * B
EPS = (1e-6, 1e-5)
GELU_SCALE = (2.0 / math.pi) ** 0.5
GELU_CUBE = 0.044715
MASKED = -float(2 ** 30)
BLOCKS = (3, 2, 1)
ROW_MASK = sum(BLOCKS) * HD
ROW_MAX = ROW_MASK + 1
ROWS = ROW_MAX + 3
BANKS = 7
LAG = 2
LEAD = 13
VW = HD + 1
CW = 32
SLOTS = 3

COLS = dict(qk0=0, qk1=4, fc1=8, mod=16, lng=28, lnb=30)
NCOLS = 32
ROWV = ("v0", "v1", "proj0", "proj1", "fc2", "gate_msa", "gate_mlp", "gamma", "beta", "ln_g", "ln_b")


def schedule():
    plan = []

    def norm(u, k):
        return [[("stats", u, k, th)] for th in range(2)] + [
            x for th in range(2) for x in ([("xn", u, k, th)], [("lnT", u, k, th, cc) for cc in range(CC)])]

    def qk(u, j):
        return [("qk", u, j), ("qk", u, j + 4)]

    def after(u):
        def half(th):
            return [[("opT", u, th, cc) for cc in range(CC)]] + pairs("proj", th)

        def pairs(kind, th):
            return [[(kind, u, t), (kind, u, t + 1)] for t in (4 * th, 4 * th + 2)]
        if u >= B:
            steps = [x for th in range(2) for x in (*half(th), [("stats", u, 1, th)], *pairs("fin", th))]
            return steps if u == UNITS - 1 else [[e] for x in steps for e in x]
        stats0, stats1, xn0, lnT0, xn1, lnT1 = norm(u, 1)
        a0, a1 = half(0), half(1)
        steps = [*a0, stats0 + a1[0], a1[1], xn0 + a1[2], lnT0 + [("bias_in", u, 1, 0)] + stats1]
        for tb in range(TB):
            f = [("fc1", u, tb, k) for k in range(4)]
            g = [("tanh", u, tb, k) for k in range(4)]
            o = [("gelu", u, tb, k) for k in range(4)]
            steps += [[f[0]], [g[0], f[1]], [o[0], g[1]], [f[2], o[1]], [g[2], f[3]], [o[2], g[3]], [o[3]],
                      [("fc2", u, tb, 0), ("fc2", u, tb, 1)]]
        n = len(steps) - 8 * TB
        steps[n + 1] += xn1 + [("bias_in", u, 1, 1)]
        steps[n + 2] += lnT1
        return steps

    def maxima(step, k):
        u, i, m = step // STEPS, step // KT % ITEMS, 4 * (step % KT) + k
        if u >= UNITS:
            return []
        return [("smax", u, i, m)] + ([("neg", u, i)] if m == 4 * KT - 1 else [])

    def max_rows(step):
        u, i = step // STEPS, step // KT % ITEMS
        return [("mrow", u, i)] if step % KT == KT - 1 and 0 <= u < UNITS else []

    stats0, stats1, xn0, lnT0, xn1, lnT1 = norm(0, 0)
    plan += [*stats0, ("silu",), *stats1, *xn0, ("mod", 0), *lnT0, ("quarter",), *xn1, *qk(0, 0)]
    plan += [*lnT1, ("qk", 0, 1), ("mask",), ("qk", 0, 5), ("load", 0, 0)]
    stats0, stats1, xn0, lnT0, xn1, lnT1 = norm(1, 0)
    plan += [*qk(0, 2), *stats0, *[("v", 0, t) for t in range(4)], *stats1, *qk(0, 3), *[("v", 0, t) for t in range(4, TT)]]
    plan += [*xn0, ("mod", 1)]
    side = [lnT0, xn1, [("qk", 1, 0)], lnT1, [("qk", 1, 4)]]
    rows = [[("rows", b, k)] for b in range(B) for k in range(2)]
    for j in (1, 5, 2, 6, 3, 7):
        side += [[("qk", 1, j)], rows.pop(0) if rows else []]
    assert LAG < LEAD
    for step in range(LEAD):
        for k in range(4):
            plan += maxima(step, k)
            if k % 2:
                plan += side.pop(0) if side else []
        plan += max_rows(step - LAG)
    for steps in side:
        plan += steps
    plan.append(("load", 0, 1))
    for u in range(UNITS):
        last = u == UNITS - 1
        side = [[], []] + (after(u - 1) if u > 0 else [])
        if u == 0:
            side += [[("rows", b, k)] for b in range(B) for k in (2, 3)]
            side += [[("bias_in", b, 0, th)] for b in range(B) for th in range(2)]
        if 0 < u < UNITS - 1:
            stats0, stats1, xn0, lnT0, xn1, lnT1 = norm(u + 1, 0)
            side[-5] += stats0
            side[-3] += xn0
            side[-2] += lnT0
            side += [stats1 + qk(u + 1, 0), xn1, lnT1, qk(u + 1, 1), [], qk(u + 1, 2), [], qk(u + 1, 3)]
            side += [[("bias_in", u + 1, 0, th)] for th in range(2)]
        if last:
            end = after(u)
            side += [[]] * (7 * KT + 2 - len(side)) + end[:6]
        for i in range(ITEMS):
            for s in range(KT):
                step = u * STEPS + i * KT + s + LEAD
                extra = list(side.pop(0)) if side else []
                if i == ITEMS - 1 and s > 0 and not last:
                    extra.append(("v", u + 1, s - 1))
                if i == 0 and s == 0 and u > 0:
                    extra.append(("v", u, KT - 1))
                if s == 1 and u * ITEMS + i > 0:
                    extra.append(("oT", *divmod(u * ITEMS + i - 1, ITEMS)))
                extra += max_rows(step - LAG)
                st = [("st", u, i, s, k) for k in range(4)]
                sm = [maxima(step, k) for k in range(4)]
                plan += [st[0], *sm[0], st[1], *sm[1], st[2], *sm[2], st[3], *sm[3], *extra]
                if u + i + s > 0:
                    n = u * STEPS + i * KT + s - 1
                    pu, pi, ps = n // STEPS, n // KT % ITEMS, n % KT
                    plan.append(("pv", pu, pi, ps))
                    if ps == KT - 1:
                        plan.append(("evac", pu, pi))
                if (u, i, s) == (0, 0, 7):
                    plan.append(("load", 0, 2))
                if (u, i, s) == (0, 1, 3):
                    plan.append(("weights",))
                if (i, s) == (0, 1) and u > 0:
                    plan.append(("load", u, 2))
                if (i, s) == (2, 1):
                    plan.append(("load", u, 3))
                if (i, s) == (5, 6) and not last:
                    plan.append(("load", u + 1, 0))
                if (i, s) == (6, 1) and not last:
                    plan.append(("load", u + 1, 1))
        assert not side, len(side)
    plan += [("pv", u, ITEMS - 1, KT - 1), ("evac", u, ITEMS - 1), ("oT", u, ITEMS - 1)]
    for steps in end[6:]:
        plan += steps
    return plan


def taker(e):
    kind = e[0]
    if kind in ("mod", "rows", "v", "oT", "proj", "fc2"):
        return "dve"
    if kind == "qk":
        return "dve" if e[1] // B == 0 and e[2] < 4 else "act"
    if kind in ("lnT", "mrow", "opT", "fc1"):
        return "act"
    return None


def splitter(e):
    return "dve" if e[1:] in ((0, 4), (0, 5)) else "pool"


def build(nc, x, cT, mask, adaT, WgT, WbT, qkvT0, qkvT1, projT0, projT1, fc1T, fc2T, cols, rows, out):
    plan = schedule()
    jobs, taken = {}, {"dve": 0, "act": 0}
    fills = [e for e in plan if taker(e) is not None or e[0] in ("st", "smax")]
    turn = {e: n for n, e in enumerate(fills)}
    for e in plan:
        if (w := taker(e)) is not None:
            taken[w] += 1
            jobs[e] = (len(jobs), w, taken[w])

    counts = {}
    seen = {}
    for e in plan:
        seen[e[0]] = seen.get(e[0], 0) + 1
        counts[e] = seen[e[0]]

    q_parts = nc.dram_tensor("q_parts", (2, 3, QH, C, QW), BF16, kind="Internal").ap()
    k_parts = nc.dram_tensor("k_parts", (2, 3, C, N), BF16, kind="Internal").ap()

    mask_rows = nc.dram_tensor("mask_rows", (3, 2, N), BF16, kind="Internal").ap()

    with ExitStack() as ctx:
        def sb(name, shape, dt=F32):
            return ctx.enter_context(nc.sbuf_tensor(name, shape, dt))

        def bank(name):
            return ctx.enter_context(nc.psum_tensor(name, [P, 512], F32))

        def sem(name):
            return ctx.enter_context(nc.semaphore(name))

        xs = sb("xs", [P, B * TT, C])
        xn = sb("xn", [P, 4, C])
        stat = sb("stat", [P, TT, 6])
        mv = sb("mv", [P, TT, 2])
        rstd = sb("rstd", [P, 2, TT])
        power = sb("power", [P, TT])
        hT = sb("hT", [P, CC, N])
        qf = sb("qf", [P, 2, 512])
        parts = sb("parts", [P, 2, 3, 512], BF16)
        qs = [sb(f"qs{i}", [P, QH, HG, QW], BF16) for i in range(SLOTS)]
        ks = [sb(f"ks{i}", [P, HG, N], BF16) for i in range(SLOTS)]
        va = sb("va", [P, KT, H, VW])
        prob = sb("prob", [P, 2, HG, QW])
        mx = sb("mx", [P, 2, HG * TQ, 2])
        negm = sb("negm", [P, 2, HG * TQ])
        mpart = sb("mpart", [P, 2, 3, HG * TQ], BF16)
        mrow = sb("mrow", [3 * HG * TQ, 2, P], BF16)
        oraw = sb("oraw", [P, 2, QW])
        rec = sb("rec", [P, 2, TQ, HG])
        otok = sb("otok", [P, TT, C])
        oT = sb("oT", [P, CC, N])
        tmp = sb("tmp", [P, 2, C])
        ge = sb("ge", [P, FC, BW])
        gi = sb("gi", [P, 2, 2, BW])
        wqkv = [sb(f"wqkv{i}", [P, CC, 3 * C]) for i in range(LAYERS)]
        wproj = [sb(f"wproj{i}", [P, CC, C]) for i in range(LAYERS)]
        wfc1 = sb("wfc1", [P, CC, MLP])
        wfc2 = sb("wfc2", [P, FC, C])
        col = sb("col", [P, NCOLS])
        row = sb("row", [P, len(ROWV), C])
        gate = sb("gate", [P, B, 4, C])
        gbias = sb("gbias", [P, B, 2, C])
        modc = sb("modc", [P, 12, B])
        l1c = sb("l1c", [P, 4, B])
        cs = sb("cs", [P, CC, B])
        sig = sb("sig", [P, 2, CC, B])
        sc = sb("sc", [P, CC, B])
        vq = sb("vq", [P, B, N], BF16)
        idf = sb("idf", [P, P])
        idb = sb("idb", [P, P], BF16)
        wada = prob[:, :, :, :].rearrange("p a h q -> p (a h q)")[:, 0:CC * 6 * C].rearrange("p (k n) -> p k n", k=CC)
        gef = ge[:, :, :].rearrange("p f t -> p (f t)")
        wg = gef[:, 0:512].rearrange("p (k n) -> p k n", k=CC)
        wb = gef[:, 512:1024].rearrange("p (k n) -> p k n", k=CC)
        scB = gef[:, 1024:1536].rearrange("p (k b n) -> p k b n", k=CC, b=B)
        cB = gef[:, 1536:2048].rearrange("p (k b n) -> p k b n", k=CC, b=B)

        m8 = oraw[:, :, :].rearrange("p t c -> p (t c)").bitcast(U8)[:, 0:B * N].rearrange("p (b n) -> p b n", b=B)
        mk8 = oraw[:, :, :].rearrange("p t c -> p (t c)").bitcast(U8)[0:B, B * N:(B + 1) * N]
        mk = otok[:, :, :].rearrange("p t c -> p (t c)").bitcast(BF16)[0:3, 0:2 * N].rearrange("p (s n) -> p s n", s=2)

        acc = bank("acc")
        banks = [bank(f"bank{i}") for i in range(BANKS)]

        x_in = [[sem(f"x_in{b}{th}") for th in range(2)] for b in range(B)]
        cond_in = sem("cond_in")
        mask_in = sem("mask_in")
        row_in = sem("row_in")
        ada_in = [sem(f"ada_in{i}") for i in range(2)]
        weight_in = {n: sem(f"weight_in_{n}") for n in ("qkv0", "qkv1", "proj0", "proj1", "fc1", "fc2")}
        identity_done = sem("identity_done")
        power_done = sem("power_done")
        ones_done = [sem(f"ones_done{i}") for i in range(SLOTS)]
        exp_cond = sem("exp_cond")
        cond_done = sem("cond_done")
        mask_filled = sem("mask_filled")
        mask_done = sem("mask_done")
        acc_cleared = sem("acc_cleared")
        mask_stored = sem("mask_stored")
        modulation_done = sem("modulation_done")
        rows_done = sem("rows_done")
        job_full = sem("job_full")
        job_act = sem("job_act")
        job_dve = sem("job_dve")
        job_out = {"act": job_act, "dve": job_dve}
        dve_self = sem("dve_self")
        pool_self = sem("pool_self")
        stats_done = sem("stats_done")
        rstd_done = sem("rstd_done")
        xn_done = sem("xn_done")
        biased = sem("biased")
        parts_done = [sem(f"parts_done{i}") for i in range(2)]
        stored = [sem(f"stored{i}") for i in range(2)]
        loaded = [sem(f"loaded{i}") for i in range(SLOTS)]
        st_full = sem("st_full")
        exp_done = sem("exp_done")
        pv_done = sem("pv_done")
        acc_out = sem("acc_out")
        mx_full = sem("mx_full")
        mx_out = sem("mx_out")
        neg_done = sem("neg_done")
        mpart_done = sem("mpart_done")
        mrow_in = [sem(f"mrow_in{i}") for i in range(2)]
        cube_done = sem("cube_done")
        tanh_done = sem("tanh_done")
        gelu_done = sem("gelu_done")
        fin_x = sem("fin_x")
        x_beta = sem("x_beta")
        out_stored = [sem(f"out_stored{k}") for k in range(4)]

        block = ctx.enter_context(nc.Block())

        def slot(u, g):
            return (u * GROUPS + g) % SLOTS

        def kind(u):
            return u if u < B else 2

        def new_mask(u, g):
            n = u * GROUPS + g
            return n < SLOTS or kind((n - SLOTS) // GROUPS) != kind(u)

        def loads(u, g):
            n = u * GROUPS + g
            before = loads(*divmod(n - SLOTS, GROUPS)) if n >= SLOTS else 0
            return before + (QH + 1) * (len(BLOCKS) + (1 if new_mask(u, g) else 0))

        def item(u, i):
            return u * ITEMS + i

        def bank_of(e):
            return banks[turn[e] % BANKS]

        def wait_bank(eng, e):
            if turn[e] >= BANKS:
                before = fills[turn[e] - BANKS]
                if before[0] == "st":
                    eng.wait_ge(exp_done, counts[before])
                elif before[0] == "smax":
                    eng.wait_ge(mx_out, counts[before])
                else:
                    job_taken(eng, before)
            return bank_of(e)

        def job_ready(eng, e):
            eng.wait_ge(job_full, jobs[e][0] + 1)
            return bank_of(e)

        def job_taken(eng, e):
            _, w, c = jobs[e]
            eng.wait_ge(job_out[w], c)

        @block.sync
        def _(sp):
            def load_x(b, th):
                sp.dma_start(xs[:, b * TT + 4 * th:b * TT + 4 * th + 4, :],
                             x[b, th * 512:(th + 1) * 512].rearrange("(t p) c -> p t c", p=P)).then_inc(x_in[b][th], 16)

            load_x(0, 0)
            load_x(0, 1)
            ada = adaT.rearrange("(k p) n -> p k n", p=P)
            sp.dma_start(wada[:, :, 0:2 * C], ada[:, :, 0:2 * C]).then_inc(ada_in[0], 16)
            sp.dma_start(wqkv[0][:, :, :], qkvT0.rearrange("(k p) n -> p k n", p=P)).then_inc(weight_in["qkv0"], 16)
            sp.dma_start(wada[:, :, 2 * C:6 * C], ada[:, :, 2 * C:6 * C]).then_inc(ada_in[1], 16)
            sp.dma_start(wg, WgT.rearrange("(k p) n -> p k n", p=P)).then_inc(ada_in[1], 16)
            sp.dma_start(wb, WbT.rearrange("(k p) n -> p k n", p=P)).then_inc(ada_in[1], 16)
            load_x(1, 0)
            load_x(1, 1)

            def load_weights():
                for name, dst, src in (("proj0", wproj[0], projT0), ("fc1", wfc1, fc1T), ("fc2", wfc2, fc2T),
                                       ("qkv1", wqkv[1], qkvT1), ("proj1", wproj[1], projT1)):
                    sp.dma_start(dst[:, :, :], src.rearrange("(k p) n -> p k n", p=P)).then_inc(weight_in[name], 16)

            def store_parts(u, j):
                n = counts[("qk", u, j)]
                sp.wait_ge(parts_done[(n - 1) % 2], (n + 1) // 2)
                if u >= 2 and j == 0:
                    for g in range(GROUPS):
                        sp.wait_ge(loaded[slot(u - 2, g)], 16 * loads(u - 2, g))
                side, cc, th = j // 4, j // 2 % 2, j % 2
                rows_ = slice(cc * P, (cc + 1) * P)
                dst = q_parts[u % 2, :, th, rows_, :] if side == 0 else k_parts[u % 2, :, rows_, th * 512:(th + 1) * 512]
                sp.dma_start(dst.rearrange("r c n -> c r n"), parts[:, (n - 1) % 2, :, :]).then_inc(stored[(n - 1) % 2], 16)

            def load_group(u, g):
                s = slot(u, g)
                jn = counts[("qk", u, 5 if g < 2 else 7)]
                for k in range(2):
                    sp.wait_ge(stored[k], 16 * (jn // 2))
                n = u * GROUPS + g
                if n == 0:
                    sp.wait_ge(mask_stored, 16)
                if n < SLOTS:
                    sp.wait_ge(ones_done[n], 1)
                if n >= SLOTS:
                    pu, pg = divmod(n - SLOTS, GROUPS)
                    sp.wait_ge(st_full, counts[("st", pu, 2 * pg + 1, 7, 3)])
                    sp.wait_ge(mx_full, counts[("smax", pu, 2 * pg + 1, 31)])
                group = slice(g * HG * HD, (g + 1) * HG * HD)
                r0 = 0
                for r, w in enumerate(BLOCKS):
                    for qh in range(QH):
                        q = q_parts[u % 2, r:r + 1, qh, group, :].rearrange("r (d h) n -> d r (h n)", d=HD)
                        sp.dma_start(qs[s][r0:r0 + w * HD, qh, :, :].rearrange("p h n -> p (h n)"),
                                     q.to_broadcast([HD, w, HG * QW])).then_inc(loaded[s], 16)
                    k = k_parts[u % 2, 0:w, group, :].rearrange("r (d h) n -> d r (h n)", d=HD)
                    sp.dma_start(ks[s][r0:r0 + w * HD, :, :].rearrange("p h n -> p (h n)"), k).then_inc(loaded[s], 16)
                    r0 += w * HD
                if new_mask(u, g):
                    m = kind(u)
                    for qh in range(QH):
                        sp.dma_start(qs[s][ROW_MASK:ROW_MASK + 1, qh, :, :],
                                     mask_rows[m:m + 1, 0:1, qh * QW:(qh + 1) * QW].to_broadcast([1, HG, QW])).then_inc(loaded[s], 16)
                    sp.dma_start(ks[s][ROW_MASK:ROW_MASK + 1, :, :],
                                 mask_rows[m:m + 1, 1:2, :].to_broadcast([1, HG, N])).then_inc(loaded[s], 16)

            def put_max(u, i):
                e = ("mrow", u, i)
                job_taken(sp, e)
                s, qh = slot(u, i // 2), i % 2
                k = item(u, i) % 2
                for part in range(3):
                    sp.dma_start(qs[s][ROW_MAX + part:ROW_MAX + part + 1, qh, :, :].rearrange("o h q -> o (h q)"),
                                 mrow[part * HG * TQ:(part + 1) * HG * TQ, k, :]).then_inc(mrow_in[k], 16)

            for e in plan:
                if e[0] == "mask":
                    sp.wait_ge(mask_done, 1)
                    sp.dma_start(mask_rows, mk).then_inc(mask_stored, 16)
                elif e[0] == "qk":
                    store_parts(e[1], e[2])
                elif e[0] == "mrow":
                    put_max(e[1], e[2])
                elif e[0] == "fin":
                    _, u, t = e
                    sp.wait_ge(fin_x, counts[e])
                    sp.dma_start(out[u % B, t * P:(t + 1) * P, :], xn[:, t % 4, :]).then_inc(out_stored[t % 4], 16)
                elif e[0] == "load":
                    load_group(e[1], e[2])
                elif e[0] == "weights":
                    load_weights()
            for k in range(4):
                sp.wait_ge(out_stored[k], 16 * B * TT // 4)

        @block.tensor
        def _(pe):
            def mod(part):
                if part == 0:
                    pe.wait_ge(cond_done, 1)
                pe.wait_ge(ada_in[part], (16, 48)[part])
                bank_ = wait_bank(pe, ("mod", part))
                chunks = ([(wada, sc, m) for m in (0, 1, 2, 3)],
                          [(wada, sc, m) for m in (6, 7, 8, 9)] + [(wg, cs, 0), (wg, cs, 1), (wb, cs, 0), (wb, cs, 1)])[part]
                for n, (w, v, m) in enumerate(chunks):
                    for k in range(CC):
                        mm = pe.matmul(bank_[:, n * B:(n + 1) * B], w[:, k, m * P:(m + 1) * P], v[:, k, :],
                                       start=(k == 0), stop=(k == CC - 1))
                mm.then_inc(job_full, 1)

            def rows_(b, n):
                bank_ = wait_bank(pe, ("rows", b, n))
                pe.wait_ge(cond_done, 2)
                w, v = ((wada[:, :, 2 * C:3 * C], scB), (wada[:, :, 5 * C:6 * C], scB), (wg, cB), (wb, cB))[n]
                for k in range(CC):
                    mm = pe.matmul(bank_[:, 0:C], v[:, k, b, :], w[:, k, :], start=(k == 0), stop=(k == CC - 1))
                mm.then_inc(job_full, 1)

            def lnT(e):
                _, u, k, th, cc = e
                bank_ = wait_bank(pe, e)
                pe.wait_ge(xn_done, 4 * counts[("xn", u, k, th)])
                for t in range(4):
                    mm = pe.transpose(bank_[:, t * P:(t + 1) * P], xn[:, t, cc * P:(cc + 1) * P], idf[:, :])
                mm.then_inc(job_full, 1)

            def qk(e):
                _, u, j = e
                side, cc, th = j // 4, j // 2 % 2, j % 2
                bank_ = wait_bank(pe, e)
                pe.wait_ge(weight_in[f"qkv{u // B}"], 16)
                job_taken(pe, ("lnT", u, 0, th, CC - 1))
                for k in range(CC):
                    mm = pe.matmul(bank_[:, :], wqkv[u // B][:, k, side * C + cc * P:side * C + (cc + 1) * P],
                                   hT[:, k, th * 512:(th + 1) * 512], start=(k == 0), stop=(k == CC - 1))
                mm.then_inc(job_full, 1)

            def v(e):
                _, u, t = e
                bank_ = wait_bank(pe, e)
                for k in range(CC):
                    mm = pe.matmul(bank_[:, 0:C], hT[:, k, t * P:(t + 1) * P], wqkv[u // B][:, k, 2 * C:3 * C],
                                   start=(k == 0), stop=(k == CC - 1))
                mm.then_inc(job_full, 1)

            def smax(e):
                _, u, i, m = e
                n = counts[e]
                h, qt, kh = m // 8, m // 2 % 4, m % 2
                s = slot(u, i // 2)
                if m == 0:
                    pe.wait_ge(loaded[s], 16 * loads(u, i // 2))
                pe.matmul(wait_bank(pe, e)[:, :], qs[s][0:ROW_MAX, i % 2, h, qt * P:(qt + 1) * P], ks[s][0:ROW_MAX, h, kh * 512:(kh + 1) * 512],
                          start=True, stop=True).then_inc(mx_full, 1)

            def mrow_(e):
                bank_ = wait_bank(pe, e)
                k = item(e[1], e[2]) % 2
                pe.wait_ge(mpart_done, item(e[1], e[2]) + 1)
                pe.matmul(bank_[0:3 * HG * TQ, 0:P], mpart[:, k, :, :].rearrange("p r c -> p (r c)"), idb[:, :],
                          start=True, stop=True).then_inc(job_full, 1)

            def st(e):
                _, u, i, s, h = e
                n = counts[e]
                sl = slot(u, i // 2)
                if s == 0 and h == 0:
                    k = item(u, i)
                    pe.wait_ge(mrow_in[k % 2], 48 * (k // 2 + 1))
                pe.matmul(wait_bank(pe, e)[:, :], ks[sl][0:ROWS, h, s * P:(s + 1) * P], qs[sl][0:ROWS, i % 2, h, :],
                          start=True, stop=True).then_inc(st_full, 1)

            def pv(e):
                _, u, i, s = e
                n = counts[e]
                pe.wait_ge(exp_done, HG * n)
                if i == 0:
                    job_taken(pe, ("v", u, s))
                if s == 0:
                    if item(u, i) > 0:
                        pe.wait_ge(acc_out, item(u, i))
                    else:
                        pe.wait_ge(acc_cleared, 1)
                for h in range(HG):
                    mm = pe.matmul(acc[h * CW:h * CW + VW, :], va[:, s, (i // 2) * HG + h, :], prob[:, (n - 1) % 2, h, :],
                                   start=(s == 0), stop=(s == KT - 1), skip_group_check=True)
                mm.then_inc(pv_done, 1)

            def oT_(e):
                bank_ = wait_bank(pe, e)
                n = item(e[1], e[2])
                pe.wait_ge(acc_out, n + 1)
                for t in range(TQ):
                    mm = pe.transpose(bank_[:, t * P:(t + 1) * P], oraw[:, n % 2, t * P:(t + 1) * P], idf[:, :])
                mm.then_inc(job_full, 1)

            def opT(e):
                _, u, th, cc = e
                bank_ = wait_bank(pe, e)
                job_taken(pe, ("oT", u, ITEMS - 2 + th))
                for t in range(4):
                    mm = pe.transpose(bank_[:, t * P:(t + 1) * P], otok[:, 4 * th + t, cc * P:(cc + 1) * P], idf[:, :])
                mm.then_inc(job_full, 1)

            def proj(e):
                _, u, t = e
                bank_ = wait_bank(pe, e)
                pe.wait_ge(weight_in[f"proj{u // B}"], 16)
                job_taken(pe, ("opT", u, t // 4, CC - 1))
                for k in range(CC):
                    mm = pe.matmul(bank_[:, 0:C], oT[:, k, t * P:(t + 1) * P], wproj[u // B][:, k, :],
                                   start=(k == 0), stop=(k == CC - 1))
                mm.then_inc(job_full, 1)

            def fc1(e):
                _, u, tb, f2 = e
                bank_ = wait_bank(pe, e)
                pe.wait_ge(weight_in["fc1"], 16)
                job_taken(pe, ("lnT", u, 1, tb // 2, CC - 1))
                for f in range(2):
                    for k in range(CC):
                        c0 = (2 * f2 + f) * P
                        mm = pe.matmul(bank_[:, f * BW:(f + 1) * BW], wfc1[:, k, c0:c0 + P], hT[:, k, tb * BW:(tb + 1) * BW],
                                       start=(k == 0), stop=(k == CC - 1))
                mm.then_inc(job_full, 1)

            def fc2(e):
                _, u, tb, t = e
                bank_ = wait_bank(pe, e)
                pe.wait_ge(weight_in["fc2"], 16)
                pe.wait_ge(gelu_done, counts[("gelu", u, tb, FC // 2 - 1)])
                for f in range(FC):
                    mm = pe.matmul(bank_[:, 0:C], ge[:, f, t * P:(t + 1) * P], wfc2[:, f, :], start=(f == 0), stop=(f == FC - 1))
                mm.then_inc(job_full, 1)

            pe.wait_ge(identity_done, 2)
            does = dict(lnT=lnT, qk=qk, v=v, smax=smax, mrow=mrow_, st=st, pv=pv, oT=oT_, opT=opT, proj=proj, fc1=fc1, fc2=fc2)
            for e in plan:
                if e[0] == "mod":
                    mod(e[1])
                elif e[0] == "rows":
                    rows_(e[1], e[2])
                elif e[0] in does:
                    does[e[0]](e)

        @block.scalar
        def _(act):
            act.dma_start(cs[:, :, :], cT.rearrange("(k p) b -> p k b", p=P)).then_inc(cond_in, 16)
            act.dma_start(col[:, :], cols).then_inc(cond_in, 16)
            act.dma_start(mk8, mask).then_inc(mask_in, 16)
            act.dma_start(m8, mask.rearrange("(o b) n -> o b n", o=1).to_broadcast([P, B, N])).then_inc(mask_in, 16)
            act.wait_ge(cond_in, 32)
            act.activation(sig[:, 0, :, :], cs[:, :, :], ACT.Exp, scale=-1.0).then_inc(exp_cond, 1)
            act.dma_start(row[:, :, :], rows.rearrange("(o r) c -> o r c", o=1).to_broadcast([P, len(ROWV), C])).then_inc(row_in, 16)

            def lnT(e):
                _, u, k, th, cc = e
                if u == 0:
                    act.wait_ge(modulation_done, k + 1)
                if u < B:
                    a, b_ = modc[:, 4 * k + 2 + cc, u % B:u % B + 1], modc[:, 4 * k + cc, u % B:u % B + 1]
                else:
                    a, b_ = l1c[:, cc, u % B:u % B + 1], l1c[:, 2 + cc, u % B:u % B + 1]
                bank_ = job_ready(act, e)
                act.activation(hT[:, cc, th * 512:(th + 1) * 512], bank_[:, :], ACT.Identity, bias=b_, scale=a).then_inc(job_act, 1)

            def qk(e):
                _, u, j = e
                n = counts[e]
                side, cc = j // 4, j // 2 % 2
                c0 = COLS[f"qk{u // B}"] + 2 * side + cc
                bank_ = job_ready(act, e)
                if n > 2:
                    act.wait_ge(parts_done[(n - 1) % 2], (n - 1) // 2)
                act.activation(qf[:, (n - 1) % 2, :], bank_[:, :], ACT.Identity, bias=col[:, c0:c0 + 1]).then_inc(job_act, 1)

            def mrow_(e):
                k = item(e[1], e[2])
                bank_ = job_ready(act, e)
                if k >= 2:
                    act.wait_ge(mrow_in[k % 2], 48 * (k // 2))
                act.activation(mrow[:, k % 2, :], bank_[0:3 * HG * TQ, 0:P], ACT.Identity).then_inc(job_act, 1)

            def st(e):
                _, u, i, s, h = e
                n = counts[e]
                step = (n - 1) // HG
                act.wait_ge(st_full, n)
                if step >= 2:
                    act.wait_ge(pv_done, step - 1)
                act.activation(prob[:, step % 2, h, :], bank_of(e)[:, :], ACT.Exp).then_inc(exp_done, 1)

            def evac(e):
                n = item(e[1], e[2])
                act.wait_ge(pv_done, KT * (n + 1))
                if n >= 2:
                    job_taken(act, ("oT", *divmod(n - 2, ITEMS)))
                act.activation(oraw[:, n % 2, :], acc[:, :], ACT.Identity).then_inc(acc_out, 1)

            def opT(e):
                _, u, th, cc = e
                bank_ = job_ready(act, e)
                act.activation(oT[:, cc, th * 512:(th + 1) * 512], bank_[:, :], ACT.Identity).then_inc(job_act, 1)

            def fc1(e):
                _, u, tb, f2 = e
                bank_ = job_ready(act, e)
                if u == 0 and tb == 0 and f2 == 0:
                    act.wait_ge(rows_done, 1)
                if tb > 0:
                    act.wait_ge(job_full, jobs[("fc2", u, tb - 1, 1)][0] + 1)
                n = counts[e]
                if n > 2:
                    act.wait_ge(gelu_done, n - 2)
                for k in range(2):
                    b_ = col[:, COLS["fc1"] + 2 * f2 + k:COLS["fc1"] + 2 * f2 + k + 1]
                    act.activation(gi[:, (n - 1) % 2, k, :], bank_[:, k * BW:(k + 1) * BW], ACT.Square, bias=b_)
                    i = act.activation(ge[:, 2 * f2 + k, :], bank_[:, k * BW:(k + 1) * BW], ACT.Identity, bias=b_)
                i.then_inc(job_act, 1)

            def tanh(e):
                n = counts[e]
                g = gi[:, (n - 1) % 2, :, :]
                act.wait_ge(cube_done, n)
                act.activation(g, g, ACT.Tanh, scale=GELU_SCALE).then_inc(tanh_done, 1)

            does = dict(lnT=lnT, mrow=mrow_, st=st, evac=evac, opT=opT, fc1=fc1, tanh=tanh)
            for e in plan:
                if e[0] in does:
                    does[e[0]](e)
                elif e[0] == "qk" and taker(e) == "act":
                    qk(e)

        @block.vector
        def _(dve):
            own = [0]

            def link(ins):
                own[0] += 1
                ins.then_inc(dve_self, 1)
                dve.wait_ge(dve_self, own[0])

            R = {n: row[:, k, :] for k, n in enumerate(ROWV)}

            def silu():
                dve.wait_ge(exp_cond, 1)
                link(dve.tensor_scalar(sig[:, 1, :, :], sig[:, 0, :, :], 1.0, None, ALU.add))
                link(dve.reciprocal(sig[:, 0, :, :], sig[:, 1, :, :]))
                dve.tensor_tensor(sc[:, :, :], cs[:, :, :], sig[:, 0, :, :], ALU.mult).then_inc(cond_done, 1)

            def quarter():
                dve.wait_ge(mask_in, 32)
                link(dve.tensor_scalar(vq[:, :, :], m8, float(HD) ** -0.5, None, ALU.mult))

            def mask_():
                dve.wait_ge(mask_filled, 2)
                dve.tensor_copy(mk[0:B, 0, :], mk8)
                dve.tensor_scalar(mk[0:B, 1, :], mk8, -1.0, -MASKED, ALU.add, ALU.mult).then_inc(mask_done, 1)
                dve.tensor_copy(scB, sc[:, :, :].rearrange("p k (b o) -> p k b o", o=1).to_broadcast([P, CC, B, P]))
                dve.tensor_copy(cB, cs[:, :, :].rearrange("p k (b o) -> p k b o", o=1).to_broadcast([P, CC, B, P])).then_inc(cond_done, 1)
                dve.memset(acc[:, :], 0.0).then_inc(acc_cleared, 1)

            def mod(part):
                bank_ = job_ready(dve, ("mod", part))
                m = slice(4 * part, 4 + 8 * part)
                w = m.stop - m.start
                bias = col[:, COLS["mod"] + m.start:COLS["mod"] + m.stop].rearrange("p (n o) -> p n o", o=1).to_broadcast([P, w, B])
                dve.tensor_tensor(modc[:, m, :], bank_[:, 0:w * B].rearrange("p (n b) -> p n b", b=B), bias, ALU.add).then_inc(job_dve, 1)
                dve.wait_ge(job_dve, jobs[("mod", part)][2])
                i = dve.tensor_scalar(modc[:, 4 * part + 2:4 * part + 4, :], modc[:, 4 * part + 2:4 * part + 4, :], 1.0, None, ALU.add)
                if part == 0:
                    i.then_inc(modulation_done, 1)
                else:
                    for cc in range(CC):
                        g, b_ = (col[:, COLS[n] + cc:COLS[n] + cc + 1] for n in ("lng", "lnb"))
                        dve.tensor_scalar(l1c[:, cc, :], modc[:, 8 + cc, :], g, None, ALU.mult)
                        link(dve.tensor_scalar(l1c[:, 2 + cc, :], modc[:, 8 + cc, :], b_, None, ALU.mult))
                    dve.tensor_tensor(l1c[:, 2:4, :], l1c[:, 2:4, :], modc[:, 10:12, :], ALU.add).then_inc(modulation_done, 1)

            def rows_(b, n):
                e = ("rows", b, n)
                bank_ = job_ready(dve, e)
                dve.wait_ge(row_in, 16)
                name = ("gate_msa", "gate_mlp", "gamma", "beta")[n]
                dve.tensor_tensor(gate[:, b, n, :], bank_[:, 0:C], R[name], ALU.add).then_inc(job_dve, 1)
                dve.wait_ge(job_dve, jobs[e][2])
                if n < 2:
                    link(dve.tensor_tensor(gbias[:, b, n, :], gate[:, b, n, :], R[("proj0", "fc2")[n]], ALU.mult))
                if n == 1:
                    link(dve.tensor_scalar(gate[:, b, n, :], gate[:, b, n, :], 0.5, None, ALU.mult))
                if n == 3:
                    link(dve.tensor_tensor(tmp[:, 0, :], gate[:, b, 2, :], R["ln_b"], ALU.mult))
                    link(dve.tensor_tensor(gate[:, b, 3, :], gate[:, b, 3, :], tmp[:, 0, :], ALU.add))
                    i = dve.tensor_tensor(gate[:, b, 2, :], gate[:, b, 2, :], R["ln_g"], ALU.mult)
                    link(i)
                    if b == B - 1:
                        dve.memset(rec[:, :, :, :], 0.0).then_inc(rows_done, 1)

            def stats(e):
                _, u, k, th = e
                b = u % B
                if k == 1 and u >= B:
                    return
                if k == 0 and u < B:
                    dve.wait_ge(x_in[b][th], 16)
                for t in range(4 * th, 4 * th + 4):
                    i = dve.bn_stats(stat[:, t, :], xs[:, b * TT + t, :])
                link(i)
                for t in range(4 * th, 4 * th + 4):
                    i = dve.bn_aggr(mv[:, t, :], stat[:, t, :])
                i.then_inc(stats_done, 1)
                dve.wait_ge(stats_done, counts[e])

            def xn_(e):
                _, u, k, th = e
                dve.wait_ge(rstd_done, counts[("stats", u, k, th)])
                n = counts[e]
                if n > 1:
                    prev = [p for p in plan[:plan.index(e)] if p[0] == "lnT"][-1]
                    dve.wait_ge(job_full, jobs[prev][0] + 1)
                if th == 0 and (before := sum(p[0] == "fin" for p in plan[:plan.index(e)])):
                    for k4 in range(4):
                        dve.wait_ge(out_stored[k4], 16 * before // 4)
                for t in range(4):
                    tt = 4 * th + t
                    dve.tensor_scalar(xn[:, t, :], xs[:, (u % B) * TT + tt, :], mv[:, tt, 0:1], rstd[:, 1, tt:tt + 1],
                                      ALU.subtract, ALU.mult).then_inc(xn_done, 1)

            def qk(e):
                _, u, j = e
                n = counts[e]
                cc, th = j // 2 % 2, j % 2
                c0 = COLS["qk0"] + cc
                bank_ = job_ready(dve, e)
                if n > 2:
                    dve.wait_ge(parts_done[(n - 1) % 2], (n - 1) // 2)
                dve.scalar_tensor_tensor(out=qf[:, (n - 1) % 2, :], in0=bank_[:, :], scalar=col[:, c0:c0 + 1],
                                         in1=vq[:, u, th * 512:(th + 1) * 512], op0=ALU.add, op1=ALU.mult).then_inc(job_dve, 1)

            def split(e):
                n = counts[e]
                k = (n - 1) % 2
                job_taken(dve, e)
                if n > 2:
                    dve.wait_ge(stored[k], 16 * ((n - 1) // 2))
                f = qf[:, k, :]
                link(dve.tensor_scalar(parts[:, k, 0, :], f, 1.0, 0.0, ALU.mult, ALU.add))
                link(dve.tensor_tensor(f, f, parts[:, k, 0, :], ALU.subtract))
                link(dve.tensor_scalar(parts[:, k, 1, :], f, 1.0, 0.0, ALU.mult, ALU.add))
                dve.tensor_tensor(parts[:, k, 2, :], f, parts[:, k, 1, :], ALU.subtract).then_inc(parts_done[k], 1)

            def v(e):
                _, u, t = e
                bank_ = job_ready(dve, e)
                if u == 0 and t == 0:
                    dve.wait_ge(row_in, 16)
                if u > 0:
                    dve.wait_ge(pv_done, counts[("pv", u - 1, ITEMS - 1, t)])
                dve.tensor_tensor(va[:, t, :, 0:HD], bank_[:, 0:C].rearrange("p (h d) -> p h d", h=H),
                                  R[f"v{u // B}"].rearrange("p (h d) -> p h d", h=H), ALU.add).then_inc(job_dve, 1)

            def smax(e):
                _, u, i, m = e
                n = counts[e]
                dve.wait_ge(mx_full, n)
                dve.tensor_reduce(mx[:, item(u, i) % 2, m // 2, m % 2:m % 2 + 1], bank_of(e)[:, :], AX.X, ALU.max).then_inc(mx_out, 1)

            def neg(e):
                k = item(e[1], e[2])
                dve.wait_ge(mx_out, counts[("smax", e[1], e[2], 31)])
                if k >= 2:
                    dve.wait_ge(mpart_done, k - 1)
                dve.tensor_reduce(negm[:, k % 2, :], mx[:, k % 2, :, :], AX.X, ALU.max, negate=True).then_inc(neg_done, 1)
                dve.wait_ge(neg_done, k + 1)

            def oT_(e):
                _, u, i = e
                k = item(u, i)
                bank_ = job_ready(dve, e)
                o = bank_[:, :].rearrange("p (t h w) -> p t h w", t=TQ, w=CW)
                r = rec[:, k % 2, :, :]
                link(dve.reciprocal(r, o[:, :, :, HD]))
                if u >= B:
                    link(dve.tensor_scalar(r, r, float(C) ** -0.5, None, ALU.mult))
                g, qh = i // 2, i % 2
                if i < 2 and u > 0:
                    dve.wait_ge(job_full, jobs[("opT", u - 1, i, CC - 1)][0] + 1)
                dst = otok[:, qh * TQ:(qh + 1) * TQ, g * HG * HD:(g + 1) * HG * HD].rearrange("p t (h d) -> p t h d", h=HG)
                dve.tensor_tensor(dst, o[:, :, :, 0:HD], r.rearrange("p t (h o) -> p t h o", o=1).to_broadcast([P, TQ, HG, HD]),
                                  ALU.mult).then_inc(job_dve, 1)

            def residual(e, t, k):
                u = e[1]
                bank_ = job_ready(dve, e)
                xt = xs[:, (u % B) * TT + t, :]
                if t % 4 == 0:
                    dve.wait_ge(biased, counts[("bias_in", u, k, t // 4)])
                if u < B:
                    link(dve.tensor_tensor(tmp[:, t % 2, :], bank_[:, 0:C], gate[:, u % B, k, :], ALU.mult))
                    dve.tensor_tensor(xt, tmp[:, t % 2, :], xt, ALU.add).then_inc(job_dve, 1)
                else:
                    dve.tensor_tensor(xt, bank_[:, 0:C], xt, ALU.add).then_inc(job_dve, 1)
                    dve.wait_ge(job_dve, jobs[e][2])
                    link(dve.bn_stats(stat[:, t, :], xt))
                    i = dve.bn_aggr(mv[:, t, :], stat[:, t, :])
                    if t % 4 == 3:
                        n = counts[("stats", u, 1, t // 4)]
                        i.then_inc(stats_done, 1)
                        dve.wait_ge(stats_done, n)
                if t % 4 == 3:
                    dve.wait_ge(job_dve, jobs[e][2])

            def gelu(e):
                _, u, tb, f2 = e
                n = counts[e]
                dve.wait_ge(tanh_done, n)
                y = ge[:, 2 * f2:2 * f2 + 2, :]
                dve.scalar_tensor_tensor(out=y, in0=gi[:, (n - 1) % 2, :, :], scalar=1.0, in1=y, op0=ALU.add,
                                         op1=ALU.mult).then_inc(gelu_done, 1)

            def fin(e):
                _, u, t = e
                b = u % B
                k = t % 4
                n = counts[e]
                if n > 4:
                    dve.wait_ge(out_stored[k], 16 * ((n - 1) // 4))
                    dve.wait_ge(fin_x, n - 4)
                link(dve.scalar_tensor_tensor(out=xn[:, k, :], in0=xs[:, b * TT + t, :], scalar=mv[:, t, 0:1], in1=gate[:, b, 2, :],
                                              op0=ALU.subtract, op1=ALU.mult))
                if t % 4 == 0:
                    dve.wait_ge(rstd_done, counts[("stats", u, 1, t // 4)])
                dve.wait_ge(x_beta, (u - B) * TT + t + 1)
                dve.scalar_tensor_tensor(out=xn[:, k, :], in0=xn[:, k, :], scalar=rstd[:, 1, t:t + 1], in1=ge[:, t, :],
                                         op0=ALU.mult, op1=ALU.add).then_inc(fin_x, 1)

            first = dict(silu=silu, quarter=quarter, mask=mask_)
            does = dict(stats=stats, xn=xn_, v=v, smax=smax, neg=neg, oT=oT_, fin=fin, gelu=gelu)
            for e in plan:
                if e[0] == "mod":
                    mod(e[1])
                elif e[0] == "rows":
                    rows_(e[1], e[2])
                elif e[0] == "proj":
                    residual(e, e[2], 0)
                elif e[0] == "fc2":
                    residual(e, 2 * e[2] + e[3], 1)
                elif e[0] == "qk":
                    if taker(e) == "dve":
                        qk(e)
                    if splitter(e) == "dve":
                        split(e)
                elif e[0] in does:
                    does[e[0]](e)
                elif e[0] in first:
                    first[e[0]]()

        @block.gpsimd
        def _(pool):
            own = [0]

            def link(ins):
                own[0] += 1
                ins.then_inc(pool_self, 1)
                pool.wait_ge(pool_self, own[0])

            link(pool.memset(idf[:, :], 0.0))
            pool.affine_select(out=idf[:, :], in_=idf[:, :], compare_op=ALU.not_equal, fill=1.0, base=0,
                               pattern=[[-1, P]], channel_multiplier=1).then_inc(identity_done, 1)
            pool.wait_ge(identity_done, 1)
            pool.tensor_copy(idb[:, :], idf[:, :]).then_inc(identity_done, 1)
            pool.wait_ge(identity_done, 2)
            pool.memset(power[:, :], -0.5).then_inc(power_done, 1)
            pool.wait_ge(power_done, 1)
            pool.memset(mk[:, 0, :], 1.0).then_inc(mask_filled, 1)
            pool.wait_ge(mask_filled, 1)
            pool.memset(mk[:, 1, :], 0.0).then_inc(mask_filled, 1)
            pool.wait_ge(mask_filled, 2)
            pool.memset(ks[0][ROW_MASK:ROWS, :, :], 1.0).then_inc(ones_done[0], 1)
            pool.wait_ge(ones_done[0], 1)

            def ones(s):
                pool.wait_ge(rstd_done, counts[("stats", 0, 0, 1)])
                if s == 2:
                    n = counts[("qk", 0, 1)]
                    pool.wait_ge(parts_done[(n - 1) % 2], (n + 1) // 2)
                pool.memset(ks[s][ROW_MASK:ROWS, :, :], 1.0).then_inc(ones_done[s], 1)
                pool.wait_ge(ones_done[s], 1)

            link(pool.memset(va[:, :, :, HD:VW], 1.0))

            def stats(e):
                _, u, k, th = e
                ts = slice(4 * th, 4 * th + 4)
                pool.wait_ge(stats_done, counts[e])
                pool.wait_ge(power_done, 1)
                readers = [p for p in plan[:plan.index(e)] if p[0] == "fin" and p[2] // 4 == th or p[0] == "xn" and p[3] == th]
                if readers and readers[-1][0] == "xn":
                    pool.wait_ge(xn_done, 4 * counts[readers[-1]])
                elif readers:
                    pool.wait_ge(fin_x, counts[readers[-1]])
                link(pool.tensor_scalar(rstd[:, 0, ts], mv[:, ts, 1], EPS[u // B], 1.0, ALU.add, ALU.mult))
                pool.tensor_tensor(rstd[:, 1, ts], rstd[:, 0, ts], power[:, ts], ALU.pow).then_inc(rstd_done, 1)

            def proj(e):
                _, u, t = e
                job_taken(pool, e)
                if u > B:
                    pool.wait_ge(fin_x, counts[("fin", u - 1, t)])
                pool.tensor_tensor(ge[:, t, :], xs[:, (u % B) * TT + t, :], gate[:, u % B, 3, :], ALU.add).then_inc(x_beta, 1)

            def split(e):
                n = counts[e]
                k = (n - 1) % 2
                job_taken(pool, e)
                if n > 2:
                    pool.wait_ge(stored[k], 16 * ((n - 1) // 2))
                f = qf[:, k, :]
                link(pool.tensor_scalar(parts[:, k, 0, :], f, 1.0, 0.0, ALU.mult, ALU.add))
                link(pool.tensor_tensor(f, f, parts[:, k, 0, :], ALU.subtract))
                link(pool.tensor_scalar(parts[:, k, 1, :], f, 1.0, 0.0, ALU.mult, ALU.add))
                pool.tensor_tensor(parts[:, k, 2, :], f, parts[:, k, 1, :], ALU.subtract).then_inc(parts_done[k], 1)

            def neg(e):
                n = item(e[1], e[2])
                k = n % 2
                pool.wait_ge(neg_done, n + 1)
                if n >= 2:
                    pool.wait_ge(job_full, jobs[("mrow", *divmod(n - 2, ITEMS))][0] + 1)
                f = negm[:, k, :]
                link(pool.tensor_scalar(mpart[:, k, 0, :], f, 1.0, 0.0, ALU.mult, ALU.add))
                link(pool.tensor_tensor(f, f, mpart[:, k, 0, :], ALU.subtract))
                link(pool.tensor_scalar(mpart[:, k, 1, :], f, 1.0, 0.0, ALU.mult, ALU.add))
                pool.tensor_tensor(mpart[:, k, 2, :], f, mpart[:, k, 1, :], ALU.subtract).then_inc(mpart_done, 1)

            def bias_in(e):
                _, u, k, th = e
                pool.wait_ge(xn_done, 4 * counts[("xn", u, k, th)])
                if u == 0 and k == 0:
                    pool.wait_ge(rows_done, 1)
                bias = gbias[:, u % B, k, :] if u < B else row[:, ROWV.index("proj1"), :]
                for t in range(4 * th, 4 * th + 4):
                    xt = xs[:, (u % B) * TT + t, :]
                    i = pool.tensor_tensor(xt, xt, bias, ALU.add)
                i.then_inc(biased, 1)

            def fc1(e):
                _, u, tb, f2 = e
                n = counts[e]
                g = gi[:, (n - 1) % 2, :, :]
                job_taken(pool, e)
                link(pool.tensor_scalar(g, g, GELU_CUBE, 1.0, ALU.mult, ALU.add))
                pool.tensor_tensor(g, g, ge[:, 2 * f2:2 * f2 + 2, :], ALU.mult).then_inc(cube_done, 1)

            does = dict(stats=stats, neg=neg, bias_in=bias_in, fc1=fc1)
            for e in plan:
                if e[0] in does:
                    does[e[0]](e)
                elif e[0] == "qk" and splitter(e) == "pool":
                    split(e)
                elif e[0] in ("quarter", "mask"):
                    ones(1 if e[0] == "quarter" else 2)
                elif e[0] == "proj" and e[1] >= B:
                    proj(e)


def kernel(**inputs):
    import numpy as np
    import concourse.bacc as bacc
    from concourse.bass_utils import run_bass_kernel_spmd

    a = {n: np.asarray(v) for n, v in inputs.items()}

    def t(w):
        return np.ascontiguousarray(w.T)

    def chunks(v):
        return v.reshape(-1, P).T

    def by_group(w):
        return w.reshape(-1, GROUPS, HG, HD).transpose(0, 1, 3, 2).reshape(-1, C)

    def grouped(w):
        return np.concatenate([by_group(w[:, :C]), by_group(w[:, C:2 * C]), w[:, 2 * C:]], axis=1)

    w1 = a["L1_cond_Wqkv"].reshape(C, 3, C).transpose(1, 0, 2).reshape(3 * C, C)
    b1 = a["L1_cond_bqkv"].reshape(C, 3).T.reshape(3 * C)
    b0, ada = a["L0_cond_qkv_b"], a["L0_cond_ada_b"].reshape(6, C)
    cols = np.concatenate([
        chunks(grouped(b0[None])[0, :2 * C]), chunks(grouped(b1[None])[0, :2 * C]), chunks(a["L0_cond_fc1_b"]),
        chunks(ada[0]), chunks(ada[1]), chunks(ada[3]), chunks(ada[4]), chunks(a["L1_cond_bg"]), chunks(a["L1_cond_bb"]),
        chunks(a["L1_cond_ln_g"]), chunks(a["L1_cond_ln_b"])], axis=1)
    rows = np.stack([b0[2 * C:], b1[2 * C:], a["L0_cond_proj_b"], a["L1_cond_bp"], a["L0_cond_fc2_b"], ada[2], ada[5],
                     a["L1_cond_bg"], a["L1_cond_bb"], a["L1_cond_ln_g"], a["L1_cond_ln_b"]])
    arrays = {
        "x": a["x"], "cT": t(a["cond_1024"]), "mask": a["mask_BxS_bk1"],
        "adaT": t(a["L0_cond_ada_w"]), "WgT": t(a["L1_cond_Wg"]), "WbT": t(a["L1_cond_Wb"]),
        "qkvT0": grouped(t(a["L0_cond_qkv_w"])), "qkvT1": grouped(t(w1)), "projT0": t(a["L0_cond_proj_w"]), "projT1": t(a["L1_cond_Wp"]),
        "fc1T": t(a["L0_cond_fc1_w"]), "fc2T": t(a["L0_cond_fc2_w"]), "cols": cols, "rows": rows,
    }
    arrays = {f"in_{n}": np.ascontiguousarray(v) for n, v in arrays.items()}
    nc = bacc.Bacc("TRN2", target_bir_lowering=False, num_devices=1)
    args = [nc.dram_tensor(n, v.shape, mybir.dt.from_np(v.dtype), kind="ExternalInput").ap() for n, v in arrays.items()]
    args.append(nc.dram_tensor("out_0", (B, N, C), F32, kind="ExternalOutput").ap())
    build(nc, *args)
    r = run_bass_kernel_spmd(nc, [arrays], core_ids=[0])
    return r.results[0]["out_0"]
```
